# Optimizing a Trainium2 kernel written in Bass

```python
import numpy as np
import jax
import jax.numpy as jnp

def _softmax(x, axis=-1):
    return jax.nn.softmax(x, axis=axis)

def _gelu(x):
    return jax.nn.gelu(x, approximate=True)

def _silu(x):
    return jax.nn.silu(x)

def _sigmoid(x):
    return jax.nn.sigmoid(x)

def _layernorm(x, axis=-1, eps=1e-05):
    m = jnp.mean(x, axis=axis, keepdims=True)
    v = jnp.var(x, axis=axis, keepdims=True)
    return (x - m) / jnp.sqrt(v + eps)

def _scatter_add(tgt, idx, src, axis=0):
    return tgt.at[idx].add(src)

def _segment_sum(src, seg, n):
    return jax.ops.segment_sum(src, seg, n)
kernel_name = 'mk_gnn_resnorm_d1_gnn_r64_1645f7'

def setup_inputs(seed: int=0):
    np.random.seed(seed)
    _w = jnp.asarray

    def _rec_inputs():
        import jax
        import jax.numpy as jnp
        _gk = jax.random.key(seed)
        x = -0.0008691 + 1 * jax.random.normal(jax.random.fold_in(_gk, 1), (100000, 128), jnp.float32)
        src = jax.random.randint(jax.random.fold_in(_gk, 2), (50000,), 0, 100000, jnp.int32)
        dst = jax.random.randint(jax.random.fold_in(_gk, 3), (50000,), 0, 100000, jnp.int32)
        _o = jnp.argsort(dst, stable=True)
        src = src[_o]
        dst = dst[_o]
        edge_attr_9 = 0.000458729 + 1.00015 * jax.random.normal(jax.random.fold_in(_gk, 11), (50000, 9), jnp.float32)
        return (x, src, dst, edge_attr_9)
    x, src, dst, edge_attr_9 = _rec_inputs()

    def _L0_gnn_setup():
        import jax, jax.numpy as jnp
        import numpy as np
        from fractions import Fraction
        from math import factorial

        def _su2_cg_coeff(j1, m1, j2, m2, j3, m3):
            if m3 != m1 + m2:
                return 0.0
            vmin = int(max(-j1 + j2 + m3, -j1 + m1, 0))
            vmax = int(min(j2 + j3 + m1, j3 - j1 + j2, j3 + m3))
            f = lambda n: factorial(round(n))
            C = ((2.0 * j3 + 1.0) * Fraction(f(j3 + j1 - j2) * f(j3 - j1 + j2) * f(j1 + j2 - j3) * f(j3 + m3) * f(j3 - m3), f(j1 + j2 + j3 + 1) * f(j1 - m1) * f(j1 + m1) * f(j2 - m2) * f(j2 + m2))) ** 0.5
            S = 0
            for v in range(vmin, vmax + 1):
                S += (-1) ** (v + j2 + m2) * Fraction(f(j2 + j3 + m1 - v) * f(j1 - m1 + v), f(v) * f(j3 - j1 + j2 - v) * f(j3 + m3 - v) * f(v + j1 - j2 - m3))
            return float(C * S)

        def _change_basis_real_to_complex(l):
            q = np.zeros((2 * l + 1, 2 * l + 1), dtype=np.complex128)
            for m in range(-l, 0):
                q[l + m, l + abs(m)] = 1 / np.sqrt(2)
                q[l + m, l - abs(m)] = -1j / np.sqrt(2)
            q[l, l] = 1
            for m in range(1, l + 1):
                q[l + m, l + abs(m)] = (-1) ** m / np.sqrt(2)
                q[l + m, l - abs(m)] = 1j * (-1) ** m / np.sqrt(2)
            return (-1j) ** l * q

        def wigner_3j(l1, l2, l3):
            C = np.zeros((2 * l1 + 1, 2 * l2 + 1, 2 * l3 + 1))
            for m1 in range(-l1, l1 + 1):
                for m2 in range(-l2, l2 + 1):
                    m3 = m1 + m2
                    if abs(m3) <= l3:
                        C[l1 + m1, l2 + m2, l3 + m3] = _su2_cg_coeff(l1, m1, l2, m2, l3, m3)
            Q1 = _change_basis_real_to_complex(l1)
            Q2 = _change_basis_real_to_complex(l2)
            Q3 = _change_basis_real_to_complex(l3)
            Cc = np.einsum('ij,kl,mn,ikn->jlm', Q1, Q2, np.conj(Q3.T), C.astype(np.complex128))
            Cr = np.real(Cc)
            return Cr / np.linalg.norm(Cr)
        MUL = 32
        IRREPS_IN = [(MUL, 0, 1), (MUL, 1, -1)]
        IRREPS_SH = [(1, 0, 1), (1, 1, -1), (1, 2, 1)]
        IRREPS_OUT = [(MUL, 0, 1), (MUL, 1, -1)]
        NUM_NEIGHBORS = 10.0
        N_NODES, N_EDGES = (10000, 100000)

        def _dim(irreps):
            return sum((m * (2 * l + 1) for m, l, _ in irreps))

        def _slices(irreps):
            s, out = (0, [])
            for m, l, _ in irreps:
                d = m * (2 * l + 1)
                out.append((s, s + d))
                s += d
            return out

        def _instructions():
            ins = []
            for i1, (m1, l1, p1) in enumerate(IRREPS_IN):
                for i2, (m2, l2, p2) in enumerate(IRREPS_SH):
                    for io, (mo, lo, po) in enumerate(IRREPS_OUT):
                        if abs(l1 - l2) <= lo <= l1 + l2 and p1 * p2 == po:
                            ins.append((i1, i2, io))
            return ins
        _INSTR = _instructions()
        _SL_IN, _SL_SH, _SL_OUT = (_slices(IRREPS_IN), _slices(IRREPS_SH), _slices(IRREPS_OUT))
        _W3J = [jnp.asarray(wigner_3j(IRREPS_IN[i1][1], IRREPS_SH[i2][1], IRREPS_OUT[io][1]), dtype=jnp.float32) for i1, i2, io in _INSTR]
        _NORM = []
        for _i1, _i2, _io in _INSTR:
            _alpha = 2 * IRREPS_OUT[_io][1] + 1
            _x = sum((IRREPS_IN[j1][0] * IRREPS_SH[j2][0] for j1, j2, jo in _INSTR if jo == _io))
            _NORM.append(float(np.sqrt(_alpha / _x)))

        def _tensor_product(x1, x2, weights):
            E = x1.shape[0]
            out = jnp.zeros((E, _dim(IRREPS_OUT)), dtype=x1.dtype)
            for k, (i1, i2, io) in enumerate(_INSTR):
                m1, l1, _ = IRREPS_IN[i1]
                m2, l2, _ = IRREPS_SH[i2]
                mo, lo, _ = IRREPS_OUT[io]
                a, b = _SL_IN[i1]
                c, d = _SL_SH[i2]
                e, f = _SL_OUT[io]
                x1s = x1[:, a:b].reshape(E, m1, 2 * l1 + 1)
                x2s = x2[:, c:d].reshape(E, m2, 2 * l2 + 1)
                seg = jnp.einsum('uvw,ijk,eui,evj->ewk', weights[k], _W3J[k], x1s, x2s, optimize='optimal') * _NORM[k]
                out = out.at[:, e:f].add(seg.reshape(E, mo * (2 * lo + 1)))
            return out
        key = jax.random.key(seed)
        ks = jax.random.split(key, 8)
        x = jax.random.normal(ks[0], (N_NODES, _dim(IRREPS_IN)), dtype=jnp.float32)
        edge_index = jax.random.randint(ks[1], (2, N_EDGES), 0, N_NODES)
        edge_attr = jax.random.normal(ks[2], (N_EDGES, _dim(IRREPS_SH)), dtype=jnp.float32)
        ws = {f'w{k}': jax.random.normal(ks[3 + k], (MUL, 1, MUL), dtype=jnp.float32) for k in range(len(_INSTR))}
        return {'x': x, 'edge_index': edge_index, 'edge_attr': edge_attr, **ws}
    _L0_gnn_all = _L0_gnn_setup()
    _L0_gnn_in = {k: v for k, v in _L0_gnn_all.items() if k in ('w0', 'w1', 'w2', 'w3', 'w4')}
    del _L0_gnn_all
    return {'x': x, 'src': src, 'dst': dst, 'edge_attr_9': edge_attr_9, 'L0_gnn_w0': _L0_gnn_in['w0'], 'L0_gnn_w1': _L0_gnn_in['w1'], 'L0_gnn_w2': _L0_gnn_in['w2'], 'L0_gnn_w3': _L0_gnn_in['w3'], 'L0_gnn_w4': _L0_gnn_in['w4']}

def reference(x, src, dst, edge_attr_9, L0_gnn_w0, L0_gnn_w1, L0_gnn_w2, L0_gnn_w3, L0_gnn_w4):
    import jax
    import jax.numpy as jnp

    def _L0_gnn_ref(x, edge_index, edge_attr, w0, w1, w2, w3, w4):
        import jax, jax.numpy as jnp
        import numpy as np
        from fractions import Fraction
        from math import factorial

        def _su2_cg_coeff(j1, m1, j2, m2, j3, m3):
            if m3 != m1 + m2:
                return 0.0
            vmin = int(max(-j1 + j2 + m3, -j1 + m1, 0))
            vmax = int(min(j2 + j3 + m1, j3 - j1 + j2, j3 + m3))
            f = lambda n: factorial(round(n))
            C = ((2.0 * j3 + 1.0) * Fraction(f(j3 + j1 - j2) * f(j3 - j1 + j2) * f(j1 + j2 - j3) * f(j3 + m3) * f(j3 - m3), f(j1 + j2 + j3 + 1) * f(j1 - m1) * f(j1 + m1) * f(j2 - m2) * f(j2 + m2))) ** 0.5
            S = 0
            for v in range(vmin, vmax + 1):
                S += (-1) ** (v + j2 + m2) * Fraction(f(j2 + j3 + m1 - v) * f(j1 - m1 + v), f(v) * f(j3 - j1 + j2 - v) * f(j3 + m3 - v) * f(v + j1 - j2 - m3))
            return float(C * S)

        def _change_basis_real_to_complex(l):
            q = np.zeros((2 * l + 1, 2 * l + 1), dtype=np.complex128)
            for m in range(-l, 0):
                q[l + m, l + abs(m)] = 1 / np.sqrt(2)
                q[l + m, l - abs(m)] = -1j / np.sqrt(2)
            q[l, l] = 1
            for m in range(1, l + 1):
                q[l + m, l + abs(m)] = (-1) ** m / np.sqrt(2)
                q[l + m, l - abs(m)] = 1j * (-1) ** m / np.sqrt(2)
            return (-1j) ** l * q

        def wigner_3j(l1, l2, l3):
            C = np.zeros((2 * l1 + 1, 2 * l2 + 1, 2 * l3 + 1))
            for m1 in range(-l1, l1 + 1):
                for m2 in range(-l2, l2 + 1):
                    m3 = m1 + m2
                    if abs(m3) <= l3:
                        C[l1 + m1, l2 + m2, l3 + m3] = _su2_cg_coeff(l1, m1, l2, m2, l3, m3)
            Q1 = _change_basis_real_to_complex(l1)
            Q2 = _change_basis_real_to_complex(l2)
            Q3 = _change_basis_real_to_complex(l3)
            Cc = np.einsum('ij,kl,mn,ikn->jlm', Q1, Q2, np.conj(Q3.T), C.astype(np.complex128))
            Cr = np.real(Cc)
            return Cr / np.linalg.norm(Cr)
        MUL = 32
        IRREPS_IN = [(MUL, 0, 1), (MUL, 1, -1)]
        IRREPS_SH = [(1, 0, 1), (1, 1, -1), (1, 2, 1)]
        IRREPS_OUT = [(MUL, 0, 1), (MUL, 1, -1)]
        NUM_NEIGHBORS = 10.0
        N_NODES, N_EDGES = (10000, 100000)

        def _dim(irreps):
            return sum((m * (2 * l + 1) for m, l, _ in irreps))

        def _slices(irreps):
            s, out = (0, [])
            for m, l, _ in irreps:
                d = m * (2 * l + 1)
                out.append((s, s + d))
                s += d
            return out

        def _instructions():
            ins = []
            for i1, (m1, l1, p1) in enumerate(IRREPS_IN):
                for i2, (m2, l2, p2) in enumerate(IRREPS_SH):
                    for io, (mo, lo, po) in enumerate(IRREPS_OUT):
                        if abs(l1 - l2) <= lo <= l1 + l2 and p1 * p2 == po:
                            ins.append((i1, i2, io))
            return ins
        _INSTR = _instructions()
        _SL_IN, _SL_SH, _SL_OUT = (_slices(IRREPS_IN), _slices(IRREPS_SH), _slices(IRREPS_OUT))
        _W3J = [jnp.asarray(wigner_3j(IRREPS_IN[i1][1], IRREPS_SH[i2][1], IRREPS_OUT[io][1]), dtype=jnp.float32) for i1, i2, io in _INSTR]
        _NORM = []
        for _i1, _i2, _io in _INSTR:
            _alpha = 2 * IRREPS_OUT[_io][1] + 1
            _x = sum((IRREPS_IN[j1][0] * IRREPS_SH[j2][0] for j1, j2, jo in _INSTR if jo == _io))
            _NORM.append(float(np.sqrt(_alpha / _x)))

        def _tensor_product(x1, x2, weights):
            E = x1.shape[0]
            out = jnp.zeros((E, _dim(IRREPS_OUT)), dtype=x1.dtype)
            for k, (i1, i2, io) in enumerate(_INSTR):
                m1, l1, _ = IRREPS_IN[i1]
                m2, l2, _ = IRREPS_SH[i2]
                mo, lo, _ = IRREPS_OUT[io]
                a, b = _SL_IN[i1]
                c, d = _SL_SH[i2]
                e, f = _SL_OUT[io]
                x1s = x1[:, a:b].reshape(E, m1, 2 * l1 + 1)
                x2s = x2[:, c:d].reshape(E, m2, 2 * l2 + 1)
                seg = jnp.einsum('uvw,ijk,eui,evj->ewk', weights[k], _W3J[k], x1s, x2s, optimize='optimal') * _NORM[k]
                out = out.at[:, e:f].add(seg.reshape(E, mo * (2 * lo + 1)))
            return out
        i, j = (edge_index[0], edge_index[1])
        summand = _tensor_product(x[i], edge_attr, [w0, w1, w2, w3, w4])
        out = jax.ops.segment_sum(summand, j, num_segments=x.shape[0])
        return out / float(np.sqrt(NUM_NEIGHBORS))
    edge_index = jnp.stack([src, dst])
    x = _layernorm(x + _L0_gnn_ref(x, edge_index, edge_attr_9, L0_gnn_w0, L0_gnn_w1, L0_gnn_w2, L0_gnn_w3, L0_gnn_w4), axis=-1)
    return x

_drawn_inputs = setup_inputs


def setup_inputs(seed=0):
    import zlib

    import numpy as np

    out = dict(_drawn_inputs(seed))
    spreads = {}
    factors = {}
    for name, (base, spread) in spreads.items():
        noise = np.random.default_rng([zlib.crc32(name.encode()), seed]).standard_normal(out[name].shape)
        drawn = base * np.exp(spread * noise) if base else spread * noise
        out[name] = jnp.asarray(drawn.astype(out[name].dtype))
    for name, factor in factors.items():
        out[name] = (out[name] * factor).astype(out[name].dtype)
    return out
```

```python
import concourse.bass as bass
from concourse import mybir
from contextlib import ExitStack

FP32 = mybir.dt.float32
BF16 = mybir.dt.bfloat16
I32 = mybir.dt.int32
ALU = mybir.AluOpType
ACT = mybir.ActivationFunctionType
AXX = mybir.AxisListType.X

P = 128
N_NODES, N_EDGES = 100000, 50000
MUL = 32
QT = 4
QE = QT * P
NQ = 98
E_PAD = NQ * QE
E_FULL = N_EDGES // P
E_TAIL = N_EDGES - E_FULL * P
OT = 8
NO = 98
LAG = 4
ROW = P + 1
TERMS = 5
COEF = 10
PARTS = 3
AP_ROWS, AP_COLS = 100, 5000
DP, DC = 125, 400
HCH = 100
HB = 32
NO_NODE = 1 << 22
EPS = 1e-5


def need(eng, sem, value):
    if isinstance(value, int) and value <= 0:
        return
    eng.wait_ge(sem, value)


def fixed(eng, value):
    return value if isinstance(value, int) else eng.snap(value)


def count(eng, value):
    return value if isinstance(value, int) else eng.to_reg(value)


def turns(q0, off, per):
    return q0 * (per // 2) + per * (off // 2 + 1)


def build(nc, x, srcT, src_tail, dst, dstT, dst_tail, attrT, w0, w1, w2, w3, w4, cst, gsel, out, FORCE=0):
    ctx = ExitStack()
    with ctx:
        def sb(name, shape, dt=FP32):
            return ctx.enter_context(nc.sbuf_tensor(name, shape, dt))

        def ps(name, shape, dt=FP32):
            return ctx.enter_context(nc.psum_tensor(name, shape, dt))

        def sem(name):
            return ctx.enter_context(nc.semaphore(name))

        msg_d = nc.dram_tensor("msg_scratch", [E_PAD, ROW], FP32, kind="Internal").ap()
        harm_d = nc.dram_tensor("harm_scratch", [PARTS * COEF, N_EDGES], BF16, kind="Internal").ap()
        lo_d = nc.dram_tensor("lo_scratch", [1, HB * HB], I32, kind="Internal").ap()

        cst_sb = sb("cst_sb", [P, 2 * P + 5 * MUL + 1])
        ident = cst_sb[:, 0:P]
        perm = cst_sb[:, P:2 * P]
        w_scale = cst_sb[:, 2 * P:2 * P + 5 * MUL]
        a_scale = cst_sb[0:AP_ROWS, 2 * P + 5 * MUL:2 * P + 5 * MUL + 1]
        gsel_f = sb("gsel_f", [PARTS * COEF, TERMS * P])
        gsel_sb = sb("gsel_sb", [PARTS * COEF, TERMS * P], BF16)
        w_raw = sb("w_raw", [P, 5 * MUL])
        w_sb = sb("w_sb", [P, 5 * MUL])
        src_tab = sb("src_tab", [P, NQ * QT], I32)
        dst_tab = sb("dst_tab", [P, NQ * QT], I32)
        dstf_tab = sb("dstf_tab", [P, NQ * QT])
        node_base = sb("node_base", [P, NO * OT])
        iota_f = sb("iota_f", [P, P])
        eps_sb = sb("eps_sb", [P, 1])
        ones_sb = sb("ones_sb", [P, 1])

        ha = sb("ha", [AP_ROWS, AP_COLS])
        hp = [sb(f"hp{i}", [AP_ROWS, AP_COLS], BF16) for i in range(PARTS)]
        dh = sb("dh", [DP, DC + 1], I32)
        qi = sb("qi", [DP, 2, DC], I32)
        qb = sb("qb", [DP, 2, DC], BF16)
        iota_b = sb("iota_b", [P, HB], BF16)
        oh = sb("oh", [DP, 2, 2, HCH, HB], BF16)
        hist = sb("hist", [HB, HB])
        pre = sb("pre", [HB, 2, HB])
        rowsum = sb("rowsum", [HB, 1])
        roff = sb("roff", [HB, 1])
        upper = sb("upper", [HB, HB])
        lo_f = sb("lo_f", [HB, HB])
        lo_i = sb("lo_i", [HB, HB], I32)
        bound = sb("bound", [HB, HB])
        bad = sb("bad", [DP, DC])
        bad2 = sb("bad2", [HB, 2, HB])
        badc = sb("badc", [P, 2])
        flag = sb("flag", [1, 1], I32)
        lo_row = sb("lo_row", [1, HB * HB], I32)

        idx = sb("idx", [P, 2, QT], I32)
        xg = sb("xg", [P, 2, QT, P])
        ht = sb("ht", [PARTS * COEF, 2, QE], BF16)
        xts = sb("xts", [P, 2, QE])
        prod = sb("prod", [P, 2, TERMS, QE])
        mts = sb("mts", [P, QE])
        mrow = sb("mrow", [P, 2, QT, ROW])
        win = sb("win", [P, 2, OT, ROW])
        dloc = sb("dloc", [P, OT])
        mask = sb("mask", [P, OT, P])
        xn = sb("xn", [P, 2, OT, P])
        y = sb("y", [P, 2, OT, P])
        on = sb("on", [P, 2, OT, P])
        st = sb("st", [P, OT, 6])
        dif = sb("dif", [P, OT])
        m2 = sb("m2", [P, OT])
        msum = sb("msum", [P, 2, OT])
        sq = sb("sq", [P, OT])
        tot = sb("tot", [P, OT])
        std = sb("std", [P, OT])
        rstd = sb("rstd", [P, 2, OT])
        nmr = sb("nmr", [P, 2, OT])

        xt_ps = ps("xt_ps", [P, QE])
        c_ps = [ps(f"c_ps{i}", [P, QE]) for i in range(2)]
        mt_ps = ps("mt_ps", [P, QE])
        m_ps = ps("m_ps", [P, QE])
        agg_ps = ps("agg_ps", [P, OT, P])
        pro_ps = ps("pro_ps", [P, P])

        s_zero = sem("s_zero")
        s_cst = sem("s_cst")
        s_w = sem("s_w")
        s_wz = sem("s_wz")
        s_wsc = sem("s_wsc")
        s_tab = sem("s_tab")
        s_dstf = sem("s_dstf")
        s_iota = sem("s_iota")
        s_ha = sem("s_ha")
        s_hs = sem("s_hs")
        s_hc = sem("s_hc")
        s_hr = sem("s_hr")
        s_hw = sem("s_hw")
        s_dh = sem("s_dh")
        s_q = sem("s_q")
        s_oh = sem("s_oh")
        s_hist = sem("s_hist")
        s_pre = sem("s_pre")
        s_roff = sem("s_roff")
        s_bad = sem("s_bad")
        s_badp = sem("s_badp")
        s_flag = sem("s_flag")
        s_lod = sem("s_lod")

        s_idx = sem("s_idx")
        s_xg = [sem(f"s_xg{i}") for i in range(2)]
        s_ht = [sem(f"s_ht{i}") for i in range(2)]
        s_xt = sem("s_xt")
        s_xtc = sem("s_xtc")
        s_coef = sem("s_coef")
        s_prod = sem("s_prod")
        s_mt = sem("s_mt")
        s_mtc = sem("s_mtc")
        s_m = sem("s_m")
        s_mc = sem("s_mc")
        s_ms = [sem(f"s_ms{i}") for i in range(2)]
        s_win = [sem(f"s_win{i}") for i in range(2)]
        s_xn = [sem(f"s_xn{i}") for i in range(2)]
        s_dl = sem("s_dl")
        s_mask = sem("s_mask")
        s_agg = sem("s_agg")
        s_add = sem("s_add")
        s_st = sem("s_st")
        s_sm = sem("s_sm")
        s_sq = sem("s_sq")
        s_tot = sem("s_tot")
        s_std = sem("s_std")
        s_rs = sem("s_rs")
        s_nm = sem("s_nm")
        s_norm = sem("s_norm")
        s_out = [sem(f"s_out{i}") for i in range(2)]

        s_cpy = sem("s_cpy")
        s_gtri = sem("s_gtri")
        s_gy = sem("s_gy")
        s_gm = sem("s_gm")
        s_gi = sem("s_gi")
        s_gg = sem("s_gg")
        s_gt = sem("s_gt")
        s_ge = sem("s_ge")
        s_gl = sem("s_gl")
        s_gc = sem("s_gc")
        s_gx = sem("s_gx")
        s_ga = sem("s_ga")
        s_gs = sem("s_gs")
        s_gsc = sem("s_gsc")

        block = ctx.enter_context(nc.Block())

        def prologue_sp(sp):
            sp.dma_start(cst_sb[:, :], cst[:, :]).then_inc(s_cst, 16)
            sp.dma_start(gsel_f[:, :], gsel[:, :]).then_inc(s_cst, 16)
            sp.dma_start(ha[0:90, :], attrT.rearrange("j (r c) -> (j r) c", c=AP_COLS)).then_inc(s_ha, 16)
            sp.dma_start(ha[90:100, :], attrT[6:7, :].rearrange("j (r c) -> (j r) c", c=AP_COLS)).then_inc(s_ha, 16)
            sp.wait_ge(s_zero, 1)
            sp.dma_start(dh[:, 0:DC], dst.rearrange("(p c) -> p c", c=DC)).then_inc(s_dh, 16)
            sp.dma_start(dh[0:DP - 1, DC:DC + 1], dst[DC:N_EDGES].rearrange("(p c) -> p c", c=DC)[:, 0:1], allow_slow_non_contiguous=True).then_inc(s_dh, 16)
            sp.dma_start(src_tab[:, 0:E_FULL], srcT[:, :]).then_inc(s_tab, 16)
            sp.dma_start(src_tab[0:E_TAIL, E_FULL:E_FULL + 1], src_tail[:, :]).then_inc(s_tab, 16)
            sp.dma_start(dst_tab[:, 0:E_FULL], dstT[:, :]).then_inc(s_tab, 16)
            sp.dma_start(dst_tab[0:E_TAIL, E_FULL:E_FULL + 1], dst_tail[:, :]).then_inc(s_tab, 16)
            sp.wait_ge(s_wz, 1)
            sp.dma_start(w_raw[0:MUL, 0:MUL], w0[:, 0, :]).then_inc(s_w, 16)
            sp.dma_start(w_raw[0:MUL, MUL:2 * MUL], w1[:, 0, :]).then_inc(s_w, 16)
            for i in range(3):
                sp.dma_start(w_raw[MUL + i:P:3, 0:MUL], w3[:, 0, :]).then_inc(s_w, 16)
                sp.dma_start(w_raw[MUL + i:P:3, MUL:2 * MUL], w4[:, 0, :]).then_inc(s_w, 16)
                sp.dma_start(w_raw[MUL + i:P:3, (2 + i) * MUL:(3 + i) * MUL], w2[:, 0, :]).then_inc(s_w, 16)
            for i in range(PARTS):
                sp.wait_ge(s_hc, i + 1)
                sp.dma_start(harm_d[i * COEF:(i + 1) * COEF, :].rearrange("j (r c) -> (j r) c", c=AP_COLS),
                             hp[i][:, :]).then_inc(s_hw, 16)
            sp.wait_ge(s_flag, 1)
            sp.dma_start(lo_d.rearrange("a (p c) -> (a p) c", c=HB), lo_i[:, :]).then_inc(s_lod, 16)
            sp.wait_ge(s_lod, 16)
            sp.dma_start(lo_row[:, :], lo_d[:, :]).then_inc(s_lod, 16)
            sp.wait_ge(s_lod, 32)
            sp.wait_ge(s_hw, 16 * PARTS)

        def prologue_pool(pool):
            g = nc.gpsimd
            g.iota(iota_f[:, :], pattern=[[1, P]], base=0, channel_multiplier=0, allow_small_or_imprecise_dtypes=True)
            g.iota(iota_b[:, :], pattern=[[1, HB]], base=0, channel_multiplier=0, allow_small_or_imprecise_dtypes=True)
            g.iota(node_base[:, :], pattern=[[P, NO * OT]], base=0, channel_multiplier=0,
                   allow_small_or_imprecise_dtypes=True)
            g.iota(bound[:, :], pattern=[[QE, HB // OT], [0, OT]], base=(LAG - 1) * QE - P,
                   channel_multiplier=QE * HB // OT, allow_small_or_imprecise_dtypes=True)
            g.memset(upper[:, :], 1.0).then_inc(s_iota, 1)
            pool.wait_ge(s_iota, 1)
            g.affine_select(out=upper[:, :], in_=upper[:, :], compare_op=ALU.is_gt, fill=0.0, base=0,
                            pattern=[[1, HB]], channel_multiplier=-1).then_inc(s_iota, 1)
            for i in range(PARTS - 1):
                pool.wait_ge(s_hc, i + 1)
                g.tensor_tensor(ha[:, :], ha[:, :], hp[i][:, :], ALU.subtract).then_inc(s_hr, 1)

        def prologue_act(act):
            act.wait_ge(s_hs, 1)
            nc.scalar.copy(hp[0][:, :], ha[:, :]).then_inc(s_hc, 1)
            for i in range(1, PARTS):
                act.wait_ge(s_hr, i)
                nc.scalar.copy(hp[i][:, :], ha[:, :]).then_inc(s_hc, 1)

        def prologue_dve(dve):
            v = nc.vector
            v.memset(src_tab[:, :], 0)
            v.memset(dst_tab[:, :], NO_NODE)
            v.memset(dh[:, :], NO_NODE).then_inc(s_zero, 1)
            v.memset(w_raw[:, :], 0.0).then_inc(s_wz, 1)
            v.memset(eps_sb[:, :], EPS)
            v.memset(ones_sb[:, :], 1.0)
            v.memset(badc[:, :], 0.0).then_inc(s_pre, 1)
            dve.wait_ge(s_cst, 32)
            dve.wait_ge(s_ha, 32)
            v.tensor_scalar(ha[:, :], ha[:, :], a_scale, None, ALU.mult).then_inc(s_hs, 1)
            dve.wait_ge(s_dh, 32)
            v.tensor_scalar(qi[:, 0, :], dh[:, 0:DC], 12, None, ALU.logical_shift_right)
            v.tensor_scalar(qi[:, 1, :], dh[:, 0:DC], 7, HB - 1, ALU.logical_shift_right,
                            ALU.bitwise_and).then_inc(s_q, 1)
            dve.wait_ge(s_q, 1)
            v.tensor_copy(qb[:, :, :], qi[:, :, :]).then_inc(s_q, 1)
            dve.wait_ge(s_iota, 2)
            dve.wait_ge(s_q, 2)
            for ch in range(DC // HCH):
                need(dve, s_hist, ch - 1)
                for d in range(2):
                    last = v.tensor_tensor(
                        oh[:, ch % 2, d, :, :],
                        iota_b[0:DP, :].unsqueeze(1).to_broadcast([DP, HCH, HB]),
                        qb[:, d, ch * HCH:(ch + 1) * HCH].unsqueeze(2).to_broadcast([DP, HCH, HB]), ALU.is_equal)
                last.then_inc(s_oh, 1)
            v.tensor_tensor(bad[:, :], dh[:, 0:DC], dh[:, 1:DC + 1], ALU.is_gt).then_inc(s_pre, 1)
            dve.wait_ge(s_tab, 64)
            v.tensor_copy(dstf_tab[:, :], dst_tab[:, :]).then_inc(s_dstf, 1)
            dve.wait_ge(s_w, 16 * 11)
            v.tensor_copy(gsel_sb[:, :], gsel_f[:, :])
            v.tensor_tensor(w_sb[:, :], w_raw[:, :], w_scale, ALU.mult).then_inc(s_wsc, 1)
            dve.wait_ge(s_pre, 2)
            v.tensor_reduce(badc[0:DP, 0:1], bad[:, :], AXX, ALU.add).then_inc(s_pre, 1)
            dve.wait_ge(s_hist, DC // HCH)
            v.tensor_copy(hist[:, :], pro_ps[0:HB, 0:HB])
            v.tensor_copy(pre[:, 0, :], pro_ps[0:HB, 0:HB])
            v.tensor_reduce(rowsum[:, :], pro_ps[0:HB, 0:HB], AXX, ALU.add).then_inc(s_pre, 1)
            dve.wait_ge(s_pre, 4)
            a, step, n = 0, 1, 4
            while step < HB:
                v.tensor_copy(pre[:, 1 - a, 0:step], pre[:, a, 0:step])
                v.tensor_tensor(pre[:, 1 - a, step:HB], pre[:, a, step:HB], pre[:, a, 0:HB - step],
                                ALU.add).then_inc(s_pre, 1)
                a, step, n = 1 - a, 2 * step, n + 1
                dve.wait_ge(s_pre, n)
            v.tensor_tensor(lo_f[:, :], pre[:, a, :], hist[:, :], ALU.subtract).then_inc(s_pre, 1)
            dve.wait_ge(s_roff, 1)
            v.tensor_copy(roff[:, :], pro_ps[0:HB, 64:65]).then_inc(s_pre, 1)
            dve.wait_ge(s_pre, n + 2)
            v.tensor_scalar(lo_f[:, :], lo_f[:, :], roff[:, 0:1], None, ALU.add).then_inc(s_pre, 1)
            dve.wait_ge(s_pre, n + 3)
            v.tensor_copy(lo_i[:, :], lo_f[:, :])
            v.tensor_scalar(bad2[:, 0, :], hist[:, :], float(P), None, ALU.is_gt)
            v.tensor_tensor(bad2[:, 1, :], lo_f[:, :], bound[:, :], ALU.is_gt).then_inc(s_pre, 1)
            dve.wait_ge(s_pre, n + 4)
            v.tensor_reduce(badc[0:HB, 1:2], bad2[:, :, :].rearrange("p a b -> p (a b)"), AXX,
                            ALU.add).then_inc(s_bad, 1)
            dve.wait_ge(s_badp, 1)
            v.tensor_scalar(flag[:, :], pro_ps[0:1, 96:97], float(FORCE), None, ALU.add).then_inc(s_flag, 1)

        def prologue_pe(pe):
            for ch in range(DC // HCH):
                pe.wait_ge(s_oh, ch + 1)
                for c in range(HCH):
                    last = nc.tensor.matmul(pro_ps[0:HB, 0:HB], oh[:, ch % 2, 0, c, :], oh[:, ch % 2, 1, c, :],
                                            start=(ch == 0 and c == 0), stop=(ch == DC // HCH - 1 and c == HCH - 1))
                last.then_inc(s_hist, 1)
            pe.wait_ge(s_pre, 4)
            nc.tensor.matmul(pro_ps[0:HB, 64:65], upper[:, :], rowsum[:, :], start=True, stop=True).then_inc(s_roff, 1)
            pe.wait_ge(s_bad, 1)
            nc.tensor.matmul(pro_ps[0:1, 96:97], badc[:, 0:1], ones_sb[:, :], start=True, stop=False)
            nc.tensor.matmul(pro_ps[0:1, 96:97], badc[:, 1:2], ones_sb[:, :], start=False, stop=True).then_inc(s_badp, 1)

        def exists(at, off, n):
            return 0 <= at + off < n

        def pool_gather(pool, q0, s):
            first = fixed(pool, (q0 + s) * QT)
            free, made = count(pool, q0 + s - 1), count(pool, q0 + s + 1)
            pool.wait_ge(s_tab, 64)
            need(pool, s_xt, free)
            nc.gpsimd.tensor_copy(idx[:, s, :], src_tab[:, bass.ds(first, QT)]).then_inc(s_idx, 1)
            pool.wait_ge(s_tab, 64)
            pool.wait_ge(s_idx, made)
            for t in range(QT):
                pool.indirect_dma_start(
                    out=xg[:, s, t, :], out_offset=None, in_=x[:, :],
                    in_offset=bass.IndirectOffsetOnAxis(ap=idx[:, s, t:t + 1], axis=0),
                    bounds_check=N_NODES - 1, oob_is_err=False).then_inc(s_xg[s], 16)

        def pe_masks(pe, o, so, tiles):
            for j in tiles:
                last = nc.tensor.matmul(agg_ps[:, j, :], mask[:, j, :], win[:, so, j, 0:P], start=True, stop=True)
            return last

        def pe_slot(pe, q0, s, at, nodes):
            q = q0 + s
            msg, node = exists(at, s, NQ), nodes and exists(at, s - LAG, NO)
            o = q - LAG
            if msg:
                pe.wait_ge(s_xg[s], turns(q0, s, 16 * QT))
                need(pe, s_xtc, q)
                for t in range(QT):
                    last = nc.tensor.transpose(xt_ps[:, t * P:(t + 1) * P], xg[:, s, t, :], ident)
                last.then_inc(s_xt, 1)
                pe.wait_ge(s_ht[s], turns(q0, s, 16))
            if node:
                pe.wait_ge(s_mask, o + 1)
                need(pe, s_add, o)
            for c in range(TERMS):
                if msg:
                    need(pe, s_prod, 5 * q + c - 1)
                    nc.tensor.matmul(c_ps[(5 * s + c) % 2][:, :], gsel_sb[:, c * P:(c + 1) * P], ht[:, s, :],
                                     start=True, stop=True).then_inc(s_coef, 1)
                if node and c >= 1:
                    last = pe_masks(pe, o, s, range(2 * c - 2, 2 * c))
                    if c == TERMS - 1:
                        last.then_inc(s_agg, 1)
            if msg:
                pe.wait_ge(s_prod, 5 * q + 5)
                need(pe, s_mtc, q)
                for c in range(4):
                    wc = w_sb[:, 0:MUL] if c == 0 else w_sb[:, MUL:2 * MUL]
                    nc.tensor.matmul(mt_ps[c * MUL:(c + 1) * MUL, :], wc, prod[:, s, c, :], start=True, stop=(c == 0),
                                     tile_position=(0, c * MUL))
                for c in range(1, 4):
                    last = nc.tensor.matmul(mt_ps[c * MUL:(c + 1) * MUL, :], w_sb[:, (1 + c) * MUL:(2 + c) * MUL],
                                            prod[:, s, 4, :], start=False, stop=True, tile_position=(0, c * MUL))
                last.then_inc(s_mt, 1)
                pe.wait_ge(s_mtc, q + 1)
                need(pe, s_mc, q)
                for t in range(QT):
                    last = nc.tensor.transpose(m_ps[:, t * P:(t + 1) * P], mts[:, t * P:(t + 1) * P], perm)
                last.then_inc(s_m, 1)

        def ln_stats(dve, yt, sl, R, n, np_=P):
            v = nc.vector
            for j in range(R):
                last = v.bn_stats(st[0:np_, j, :], yt[:, j, :])
            last.then_inc(s_st, 1)
            dve.wait_ge(s_st, n + 1)
            v.tensor_tensor(dif[0:np_, 0:R], st[0:np_, 0:R, 1], st[0:np_, 0:R, 4], ALU.subtract)
            v.tensor_tensor(m2[0:np_, 0:R], st[0:np_, 0:R, 2], st[0:np_, 0:R, 5], ALU.add)
            v.tensor_tensor(msum[0:np_, sl, 0:R], st[0:np_, 0:R, 1], st[0:np_, 0:R, 4], ALU.add).then_inc(s_sm, 1)
            dve.wait_ge(s_sm, n + 1)
            v.scalar_tensor_tensor(sq[0:np_, 0:R], dif[0:np_, 0:R], float(P // 4), dif[0:np_, 0:R], ALU.mult,
                                   ALU.mult).then_inc(s_sq, 1)
            dve.wait_ge(s_sq, n + 1)
            v.tensor_tensor(tot[0:np_, 0:R], m2[0:np_, 0:R], sq[0:np_, 0:R], ALU.add).then_inc(s_tot, 1)

        def ln_std(act, R, n, np_=P):
            act.wait_ge(s_tot, n + 1)
            nc.scalar.activation(std[0:np_, 0:R], tot[0:np_, 0:R], ACT.Sqrt, bias=eps_sb[0:np_, :],
                                 scale=1.0 / P).then_inc(s_std, 1)

        def ln_shift(dve, sl, R, n, np_=P):
            dve.wait_ge(s_std, n + 1)
            nc.vector.reciprocal(rstd[0:np_, sl, 0:R], std[0:np_, 0:R]).then_inc(s_rs, 1)
            dve.wait_ge(s_rs, n + 1)
            nc.vector.scalar_tensor_tensor(nmr[0:np_, sl, 0:R], msum[0:np_, sl, 0:R], -0.5, rstd[0:np_, sl, 0:R],
                                           ALU.mult, ALU.mult).then_inc(s_nm, 1)

        def ln_apply(ot, yt, sl, R, np_=P):
            for j in range(R):
                last = nc.scalar.activation(ot[:, j, :], yt[:, j, :], ACT.Identity, bias=nmr[0:np_, sl, j:j + 1],
                                            scale=rstd[0:np_, sl, j:j + 1])
            last.then_inc(s_norm, 1)

        def dve_slot(dve, q0, s, at, nodes):
            q = q0 + s
            o = q - LAG
            v = nc.vector
            for c in range(TERMS):
                if exists(at, s, NQ):
                    if c == 0:
                        dve.wait_ge(s_xtc, q + 1)
                        need(dve, s_mt, q - 1)
                    dve.wait_ge(s_coef, 5 * q + c + 1)
                    v.tensor_tensor(prod[:, s, c, :], xts[:, s, :], c_ps[(5 * s + c) % 2][:, :],
                                    ALU.mult).then_inc(s_prod, 1)
                if c == 0 and nodes and exists(at, s - LAG - 1, NO):
                    ln_shift(dve, 1 - s, OT, o - 1)
            if nodes and exists(at, s - LAG, NO):
                dve.wait_ge(s_xn[s], turns(q0, s - LAG, 16) + (16 if at + s - LAG == NO - 1 else 0))
                need(dve, s_norm, o - 1)
                dve.wait_ge(s_agg, o + 1)
                h = OT // 2
                v.tensor_tensor(y[:, s, 0:h, :], xn[:, s, 0:h, :], agg_ps[:, 0:h, :], ALU.add)
                v.tensor_tensor(y[:, s, h:OT, :], xn[:, s, h:OT, :], agg_ps[:, h:OT, :], ALU.add).then_inc(s_add, 1)
                dve.wait_ge(s_add, o + 1)
                ln_stats(dve, y[:, s, :, :], s, OT, o)
            if nodes and exists(at, s - LAG + 1, NO):
                need(dve, s_agg, o + 1)
                dve.wait_ge(s_win[1 - s], turns(q0, s - LAG + 1, 16 * OT))
                v.tensor_tensor(dloc[:, :], win[:, 1 - s, :, P], node_base[:, bass.ds((o + 1) * OT, OT)],
                                ALU.subtract).then_inc(s_dl, 1)
                dve.wait_ge(s_dl, o + 2)
                v.tensor_tensor(mask[:, :, :], iota_f[:, :].unsqueeze(1).to_broadcast([P, OT, P]),
                                dloc[:, :].unsqueeze(2).to_broadcast([P, OT, P]), ALU.is_equal).then_inc(s_mask, 1)

        def act_slot(act, q0, s, at, nodes):
            q = q0 + s
            o = q - LAG
            msg = exists(at, s, NQ)
            if msg:
                need(act, s_prod, 5 * (q - 1))
                act.wait_ge(s_xt, q + 1)
                nc.scalar.copy(xts[:, s, :], xt_ps[:, :]).then_inc(s_xtc, 1)
            if nodes and exists(at, s - LAG - 1, NO):
                need(act, s_out[1 - s], turns(q0, s - LAG - 3, 16))
                act.wait_ge(s_nm, o)
                ln_apply(on[:, 1 - s, :, :], y[:, 1 - s, :, :], 1 - s, OT)
            if msg:
                need(act, s_m, q)
                act.wait_ge(s_mt, q + 1)
                nc.scalar.copy(mts[:, :], mt_ps[:, :]).then_inc(s_mtc, 1)
                act.wait_ge(s_m, q + 1)
                need(act, s_ms[s], turns(q0, s - 2, 16))
                act.wait_ge(s_dstf, 1)
                nc.scalar.copy(mrow[:, s, :, P], dstf_tab[:, bass.ds(q * QT, QT)])
                nc.scalar.copy(mrow[:, s, :, 0:P], m_ps[:, :].rearrange("p (t f) -> p t f", f=P)).then_inc(s_mc, 1)
            if nodes and exists(at, s - LAG, NO):
                ln_std(act, OT, o)

        def oct_io(sp, o, last, dram, load, buf, done):
            def move(rows, tile):
                sp.dma_start(*((tile, rows) if load else (rows, tile))).then_inc(done, 16)
            if not last:
                move(dram[bass.ds(o, OT * P), :].rearrange("(j p) d -> p j d", p=P), buf[:, :, :])
                return
            first = (NO - 1) * OT * P
            full = (N_NODES - first) // P
            rest = N_NODES - first - full * P
            move(dram[first:first + full * P, :].rearrange("(j p) d -> p j d", p=P), buf[:, 0:full, :])
            move(dram[first + full * P:N_NODES, :], buf[0:rest, full, :])

        def sp_slot(sp, q0, s, at, nodes):
            q = q0 + s
            o = q - LAG
            if exists(at, s + 1, NQ):
                cols = fixed(sp, (q + 1) * QE)
                need(sp, s_coef, 5 * q)
                if at + s + 1 < NQ - 1:
                    sp.dma_start(ht[:, 1 - s, :], harm_d[:, bass.ds(cols, QE)]).then_inc(s_ht[1 - s], 16)
                else:
                    sp.dma_start(ht[:, 1 - s, 0:N_EDGES - cols], harm_d[:, cols:N_EDGES]).then_inc(s_ht[1 - s], 16)
            if nodes and exists(at, s - LAG + 1, NO):
                _, los = nc.values_load_multi_w_load_instructions(
                    lo_row[0:1, bass.ds((o + 1) * OT, OT)], engines=[mybir.EngineType.SP], min_val=0,
                    max_val=N_EDGES)
                rows = fixed(sp, (o + 1) * OT * P)
                stored = count(sp, turns(q0, s - 1, 16)) if exists(at, s - 1, NQ) else 16 * (NQ // 2)
                stored2 = count(sp, turns(q0, s - 2, 16)) if exists(at, s - 2, NQ) else 16 * (NQ // 2)
                used = count(sp, o)
                sp.wait_ge(s_ms[1 - s], stored)
                sp.wait_ge(s_ms[s], stored2)
                need(sp, s_agg, used)
                for j in range(OT):
                    sp.dma_start(win[:, 1 - s, j, :], msg_d[bass.ds(los[j], P), :]).then_inc(s_win[1 - s], 16)
                need(sp, s_add, used)
                oct_io(sp, rows, at + s - LAG + 1 == NO - 1, x, True, xn[:, 1 - s, :, :], s_xn[1 - s])
            if nodes and exists(at, s - LAG - 1, NO):
                rows = fixed(sp, (o - 1) * OT * P)
                sp.wait_ge(s_norm, o)
                oct_io(sp, rows, at + s - LAG - 1 == NO - 1, out, False, on[:, 1 - s, :, :], s_out[1 - s])
            if exists(at, s, NQ):
                rows = fixed(sp, q * QE)
                sp.wait_ge(s_mc, q + 1)
                sp.dma_start(msg_d[bass.ds(rows, QE), :].rearrange("(t p) d -> p t d", p=P),
                             mrow[:, s, :, :]).then_inc(s_ms[s], 16)

        def run(eng, slot, nodes):
            lead = LAG + 4
            for q0 in range(0, lead, 2):
                for s in range(2):
                    slot(eng, q0, s, q0, nodes)
            with eng.Fori(lead, NQ - 3, 2) as q0:
                for s in range(2):
                    slot(eng, q0, s, lead, nodes)
            for q0 in range(NQ - 2, NQ + (LAG + 2 if nodes else 0), 2):
                for s in range(2):
                    slot(eng, q0, s, q0, nodes)

        def run_pool(pool):
            for s in range(2):
                pool_gather(pool, 0, s)
            with pool.Fori(2, NQ - 1, 2) as q0:
                for s in range(2):
                    pool_gather(pool, q0, s)

        NT = E_PAD // P
        edge_m = win[:, 0, 0, 0:P]
        edge_d = win[:, 0, 0, P:P + 1]
        d_wide, same, earlier, below = (mask[:, i, :] for i in range(4))
        rows_y = xn[:, 0, 0, :]
        CP = 125

        def general_sp(sp):
            sp.dma_start(out.rearrange("(a b) d -> a (b d)", b=CP), x.rearrange("(a b) d -> a (b d)", b=CP)).then_inc(s_cpy, 16)
            sp.wait_ge(s_ms[0], 16 * (NQ // 2))
            sp.wait_ge(s_ms[1], 16 * (NQ // 2))

            def load(t, last):
                rows = fixed(sp, t * P)
                need(sp, s_gsc, last)
                sp.dma_start(win[:, 0, 0, :], msg_d[bass.ds(rows, P), :]).then_inc(s_gm, 16)
            load(0, 0)
            with sp.Fori(1, NT) as t:
                load(t, count(sp, t * 16))

            def normalise(o, is_last):
                rows, stored, n = fixed(sp, o * OT * P), count(sp, o * 16), count(sp, o + 1)
                need(sp, s_out[0], stored)
                oct_io(sp, rows, is_last, out, True, y[:, 0, :, :], s_xn[0])
                sp.wait_ge(s_norm, n)
                oct_io(sp, rows, is_last, out, False, on[:, 0, :, :], s_out[0])
            sp.wait_ge(s_gsc, 16 * NT)
            normalise(0, False)
            with sp.Fori(1, NO - 1) as o:
                normalise(o, False)
            normalise(NO - 1, True)
            sp.wait_ge(s_out[0], 16 * (NO + 1))

        def general_pool(pool):
            nc.gpsimd.memset(below, 1.0).then_inc(s_gtri, 1)
            pool.wait_ge(s_gtri, 1)
            nc.gpsimd.affine_select(out=below, in_=below, compare_op=ALU.is_gt, fill=0.0, base=0,
                                    pattern=[[-1, P]], channel_multiplier=1).then_inc(s_gtri, 1)
            pool.wait_ge(s_cpy, 16)
            with pool.Fori(0, NT) as t:
                n = count(pool, t + 1)
                pool.wait_ge(s_gy, 1)
                pool.wait_ge(s_gi, n)
                pool.indirect_dma_start(out=rows_y, out_offset=None, in_=out[:, :],
                                        in_offset=bass.IndirectOffsetOnAxis(ap=idx[:, 0, 0:1], axis=0),
                                        bounds_check=N_NODES - 1, oob_is_err=False).then_inc(s_gg, 16)
                pool.wait_ge(s_gy, 1)
                pool.wait_ge(s_gx, n)
                pool.wait_ge(s_gs, n)
                pool.indirect_dma_start(out=out[:, :], out_offset=bass.IndirectOffsetOnAxis(ap=idx[:, 1, 0:1], axis=0),
                                        in_=rows_y, in_offset=None,
                                        bounds_check=N_NODES - 1, oob_is_err=False).then_inc(s_gsc, 16)
                pool.wait_ge(s_gsc, t * 16 + 16)

        def general_pe(pe):
            with pe.Fori(0, NT) as t:
                pe.wait_ge(s_gi, t + 1)
                nc.tensor.transpose(pro_ps[:, :], d_wide, ident).then_inc(s_gt, 1)
                pe.wait_ge(s_ge, t + 1)
                nc.tensor.matmul(agg_ps[:, 0, :], same, edge_m, start=True, stop=True).then_inc(s_ga, 1)

        def general_dve(dve):
            v = nc.vector
            v.memset(rows_y, 0.0).then_inc(s_gy, 1)
            dve.wait_ge(s_gtri, 2)
            with dve.Fori(0, NT) as t:
                dve.wait_ge(s_gm, t * 16 + 16)
                v.tensor_copy(idx[:, 0, 0:1], edge_d)
                v.tensor_copy(d_wide, edge_d.to_broadcast([P, P])).then_inc(s_gi, 1)
                dve.wait_ge(s_gi, t + 1)
                dve.wait_ge(s_gt, t + 1)
                v.tensor_tensor(same, pro_ps[:, :], d_wide, ALU.is_equal).then_inc(s_ge, 1)
                dve.wait_ge(s_ge, t + 1)
                v.tensor_tensor(earlier, same, below, ALU.mult).then_inc(s_gl, 1)
                dve.wait_ge(s_gl, t + 1)
                v.tensor_reduce(dloc[:, 0:1], earlier, AXX, ALU.add).then_inc(s_gc, 1)
                dve.wait_ge(s_gc, t + 1)
                v.scalar_tensor_tensor(idx[:, 1, 0:1], dloc[:, 0:1], float(1 << 17), edge_d, ALU.mult,
                                       ALU.add).then_inc(s_gx, 1)
                dve.wait_ge(s_gg, t * 16 + 16)
                dve.wait_ge(s_ga, t + 1)
                v.tensor_tensor(rows_y, rows_y, agg_ps[:, 0, :], ALU.add).then_inc(s_gs, 1)
            with dve.Fori(0, NO - 1) as o:
                dve.wait_ge(s_xn[0], o * 16 + 16)
                ln_stats(dve, y[:, 0, :, :], 0, OT, o)
                ln_shift(dve, 0, OT, o)
            dve.wait_ge(s_xn[0], 16 * (NO + 1))
            ln_stats(dve, y[:, 0, :, :], 0, OT, NO - 1)
            ln_shift(dve, 0, OT, NO - 1)

        def general_act(act):
            with act.Fori(0, NO) as o:
                ln_std(act, OT, o)
                act.wait_ge(s_nm, o + 1)
                ln_apply(on[:, 0, :, :], y[:, 0, :, :], 0, OT)

        def ways(eng, fast, slow):
            eng.wait_ge(s_flag, 1)
            f = eng.value_load(flag[0:1, 0:1], min_val=0, max_val=1 << 20)
            with eng.If(f == 0):
                fast()
            with eng.Else():
                slow()

        @block.sync
        def _(sp):
            prologue_sp(sp)
            sp.dma_start(ht[:, 0, :], harm_d[:, 0:QE]).then_inc(s_ht[0], 16)

            def fast():
                run(sp, sp_slot, True)
                sp.wait_ge(s_out[0], 16 * (NO // 2))
                sp.wait_ge(s_out[1], 16 * (NO // 2) + 16)

            def slow():
                run(sp, sp_slot, False)
                general_sp(sp)
            ways(sp, fast, slow)

        @block.gpsimd
        def _(pool):
            prologue_pool(pool)

            def slow():
                run_pool(pool)
                general_pool(pool)
            ways(pool, lambda: run_pool(pool), slow)

        @block.scalar
        def _(act):
            prologue_act(act)

            def slow():
                run(act, act_slot, False)
                general_act(act)
            ways(act, lambda: run(act, act_slot, True), slow)

        @block.vector
        def _(dve):
            prologue_dve(dve)

            def slow():
                run(dve, dve_slot, False)
                general_dve(dve)
            ways(dve, lambda: run(dve, dve_slot, True), slow)

        @block.tensor
        def _(pe):
            prologue_pe(pe)
            pe.wait_ge(s_cst, 32)
            pe.wait_ge(s_wsc, 1)

            def slow():
                run(pe, pe_slot, False)
                general_pe(pe)
            ways(pe, lambda: run(pe, pe_slot, True), slow)


def wigner_3j(l1, l2, l3):
    import numpy as np
    from math import factorial

    def coeff(j1, m1, j2, m2, j3, m3):
        if m3 != m1 + m2:
            return 0.0
        vmin = int(max(-j1 + j2 + m3, -j1 + m1, 0))
        vmax = int(min(j2 + j3 + m1, j3 - j1 + j2, j3 + m3))
        f = factorial
        c = ((2.0 * j3 + 1.0) * (f(j3 + j1 - j2) * f(j3 - j1 + j2) * f(j1 + j2 - j3) * f(j3 + m3) * f(j3 - m3))
             / (f(j1 + j2 + j3 + 1) * f(j1 - m1) * f(j1 + m1) * f(j2 - m2) * f(j2 + m2))) ** 0.5
        s = 0
        for v in range(vmin, vmax + 1):
            s += ((-1) ** (v + j2 + m2) * (f(j2 + j3 + m1 - v) * f(j1 - m1 + v))
                  / (f(v) * f(j3 - j1 + j2 - v) * f(j3 + m3 - v) * f(v + j1 - j2 - m3)))
        return float(c * s)

    def basis(l):
        q = np.zeros((2 * l + 1, 2 * l + 1), dtype=np.complex128)
        for m in range(-l, 0):
            q[l + m, l + abs(m)] = 1 / np.sqrt(2)
            q[l + m, l - abs(m)] = -1j / np.sqrt(2)
        q[l, l] = 1
        for m in range(1, l + 1):
            q[l + m, l + abs(m)] = (-1) ** m / np.sqrt(2)
            q[l + m, l - abs(m)] = 1j * (-1) ** m / np.sqrt(2)
        return (-1j) ** l * q

    c = np.zeros((2 * l1 + 1, 2 * l2 + 1, 2 * l3 + 1))
    for m1 in range(-l1, l1 + 1):
        for m2 in range(-l2, l2 + 1):
            if abs(m1 + m2) <= l3:
                c[l1 + m1, l2 + m2, l3 + m1 + m2] = coeff(l1, m1, l2, m2, l3, m1 + m2)
    cc = np.einsum("ij,kl,mn,ikn->jlm", basis(l1), basis(l2), np.conj(basis(l3).T), c.astype(np.complex128))
    cr = np.real(cc)
    return cr / np.linalg.norm(cr)


def constants():
    import numpy as np
    neighbors = 10.0
    norm = {0: np.sqrt(1 / (2 * MUL)) / np.sqrt(neighbors), 1: np.sqrt(3 / (3 * MUL)) / np.sqrt(neighbors)}
    w000, w011, w101, w110, w121 = (wigner_3j(*l) for l in ((0, 0, 0), (0, 1, 1), (1, 0, 1), (1, 1, 0), (1, 2, 1)))
    t = np.abs(w121[0, 0, :]).max() or np.abs(w121[0, 1, :]).max()
    w_scale = np.zeros((P, 5 * MUL))
    g = np.zeros((COEF, TERMS, P))
    V = [slice(MUL + i, P, 3) for i in range(3)]
    w_scale[:MUL, :MUL] = norm[0] * w000[0, 0, 0]
    g[0, 0, :MUL] = 1
    w_scale[MUL:, :MUL] = norm[0] * w110[0, 0, 0]
    w_scale[:MUL, MUL:2 * MUL] = norm[1] * w011[0, 0, 0]
    w_scale[MUL:, MUL:2 * MUL] = norm[1] * t
    w_scale[MUL:, 2 * MUL:] = norm[1] * w101[0, 0, 0]
    g[0, 4, MUL:] = 1
    for i in range(3):
        for j in range(3):
            g[1 + j, 0, V[i]] = w110[i, j, 0] / w110[0, 0, 0]
        for k in range(3):
            g[1 + i, 1 + k, :MUL] = w011[0, i, k] / w011[0, 0, 0]
            for j in range(5):
                row, by = (9, np.sqrt(3)) if j == 2 else (4 + j, 1)
                g[row, 1 + k, V[i]] = w121[i, j, k] / t * by
    whole = np.rint(g)
    assert np.abs(g - whole).max() < 1e-9 and np.abs(whole).max() <= 2
    gsel = np.tile(whole.reshape(COEF, TERMS * P), (PARTS, 1)).astype(np.float32)
    ident = np.eye(P)
    perm = np.zeros((P, P))
    perm[np.arange(MUL), np.arange(MUL)] = 1
    for k in range(3):
        for w in range(MUL):
            perm[MUL + k * MUL + w, MUL + 3 * w + k] = 1
    a_scale = np.ones((P, 1))
    a_scale[90:AP_ROWS] = 1 / np.sqrt(3)
    cst = np.concatenate([ident, perm, w_scale, a_scale], axis=1).astype(np.float32)
    return cst, gsel


def host_layout(inputs):
    import numpy as np
    x, src, dst, attr = (np.asarray(inputs[n]) for n in ("x", "src", "dst", "edge_attr_9"))
    full = E_FULL * P
    cst, gsel = constants()
    arrays = {
        "x": x,
        "srcT": src[:full].reshape(E_FULL, P).T, "src_tail": src[full:].reshape(E_TAIL, 1),
        "dst": dst,
        "dstT": dst[:full].reshape(E_FULL, P).T, "dst_tail": dst[full:].reshape(E_TAIL, 1),
        "attrT": attr.T,
        **{f"w{i}": np.asarray(inputs[f"L0_gnn_w{i}"]) for i in range(5)},
        "cst": cst, "gsel": gsel,
    }
    return {n: np.ascontiguousarray(a) for n, a in arrays.items()}


def kernel(**inputs):
    import numpy as _np
    import concourse.bacc as _bacc
    from concourse import mybir as _mybir
    from concourse.bass_utils import run_bass_kernel_spmd as _run

    nc = _bacc.Bacc("TRN2", target_bir_lowering=False, num_devices=1)
    arrays = host_layout(inputs)
    args = [nc.dram_tensor(n, a.shape, _mybir.dt.from_np(a.dtype), kind="ExternalInput").ap()
            for n, a in arrays.items()]
    args.append(nc.dram_tensor("out", (N_NODES, P), _mybir.dt.float32, kind="ExternalOutput").ap())
    build(nc, *args)
    r = _run(nc, [arrays], core_ids=[0])
    return r.results[0]["out"]
```

```python
import concourse.bass as bass
from concourse import mybir
from contextlib import ExitStack

FP32 = mybir.dt.float32
BF16 = mybir.dt.bfloat16
I32 = mybir.dt.int32
ALU = mybir.AluOpType
ACT = mybir.ActivationFunctionType
AXX = mybir.AxisListType.X

P = 128
N_NODES, N_EDGES = 100000, 50000
MUL = 32
QT = 4
QE = QT * P
NQ = 98
E_PAD = NQ * QE
E_FULL = N_EDGES // P
E_TAIL = N_EDGES - E_FULL * P
OT = 8
NO = 98
LAG = 5
STORED = 1
ROW = P + 1
TERMS = 5
COEF = 10
PARTS = 3
AP_HALF = 2500
AP_ROWS, AP_COLS = 100, 5000
DP, DC = 125, 400
HCH = 100
HB = 32
NO_NODE = 1 << 22
EPS = 1e-5


def need(eng, sem, value):
    if isinstance(value, int) and value <= 0:
        return
    eng.wait_ge(sem, value)


def fixed(eng, value):
    return value if isinstance(value, int) else eng.snap(value)


def count(eng, value):
    return value if isinstance(value, int) else eng.to_reg(value)


def turns(q0, off, per):
    return q0 * (per // 2) + per * (off // 2 + 1)


def build(nc, x, srcT, src_tail, dst, dstT, dst_tail, attrT, w0, w1, w2, w3, w4, cst, gsel, out, FORCE=0):
    ctx = ExitStack()
    with ctx:
        def sb(name, shape, dt=FP32):
            return ctx.enter_context(nc.sbuf_tensor(name, shape, dt))

        def ps(name, shape, dt=FP32):
            return ctx.enter_context(nc.psum_tensor(name, shape, dt))

        def sem(name):
            return ctx.enter_context(nc.semaphore(name))

        msg_d = nc.dram_tensor("msg_scratch", [E_PAD, ROW], FP32, kind="Internal").ap()
        harm_d = nc.dram_tensor("harm_scratch", [PARTS * COEF, N_EDGES], BF16, kind="Internal").ap()
        lo_d = nc.dram_tensor("lo_scratch", [1, HB * HB], I32, kind="Internal").ap()

        cst_sb = sb("cst_sb", [P, 2 * P + 5 * MUL + 1])
        ident = cst_sb[:, 0:P]
        perm = cst_sb[:, P:2 * P]
        w_scale = cst_sb[:, 2 * P:2 * P + 5 * MUL]
        a_scale = cst_sb[0:AP_ROWS, 2 * P + 5 * MUL:2 * P + 5 * MUL + 1]
        gsel_f = sb("gsel_f", [PARTS * COEF, TERMS * P])
        gsel_sb = sb("gsel_sb", [PARTS * COEF, TERMS * P], BF16)
        w_raw = sb("w_raw", [P, 5 * MUL])
        w_sb = sb("w_sb", [P, 5 * MUL])
        src_tab = sb("src_tab", [P, NQ * QT], I32)
        dst_tab = sb("dst_tab", [P, NQ * QT], I32)
        dstf_tab = sb("dstf_tab", [P, NQ * QT])
        node_base = sb("node_base", [P, NO * OT])
        iota_f = sb("iota_f", [P, P])
        eps_sb = sb("eps_sb", [P, 1])
        quarter = sb("quarter", [P, OT])
        ones_sb = sb("ones_sb", [P, 1])

        ha = sb("ha", [AP_ROWS, AP_COLS])
        hp = [sb(f"hp{i}", [AP_ROWS, AP_COLS], BF16) for i in range(PARTS)]
        dh = sb("dh", [DP, DC + 1], I32)
        qi = sb("qi", [DP, 2, DC], I32)
        qb = sb("qb", [DP, 2, DC], BF16)
        iota_b = sb("iota_b", [DP, HB, HCH], BF16)
        oh = sb("oh", [DP, 2, 2, HB, HCH], BF16)
        hist = sb("hist", [HB, HB])
        pre = sb("pre", [HB, 2, HB])
        rowsum = sb("rowsum", [HB, 1])
        roff = sb("roff", [HB, 1])
        upper = sb("upper", [HB, HB])
        lo_f = sb("lo_f", [HB, HB])
        lo_i = sb("lo_i", [HB, HB], I32)
        bound = sb("bound", [HB, HB])
        bad = sb("bad", [DP, DC])
        bad2 = sb("bad2", [HB, 2, HB])
        badc = sb("badc", [P, 2])
        flag = sb("flag", [1, 1], I32)
        lo_row = sb("lo_row", [1, HB * HB], I32)

        idx = sb("idx", [P, 2, QT], I32)
        xg = sb("xg", [P, 2, QT, P])
        ht = sb("ht", [PARTS * COEF, 2, QE], BF16)
        xts = sb("xts", [P, 2, QE])
        prod = sb("prod", [P, 2, TERMS, QE])
        mts = sb("mts", [P, QE])
        mrow = sb("mrow", [P, 2, QT, ROW])
        win = sb("win", [P, 2, OT, ROW])
        dloc = sb("dloc", [P, 2, OT])
        mask = sb("mask", [P, 2, OT, P])
        xn = sb("xn", [P, 2, OT, P])
        y = sb("y", [P, 2, OT, P])
        on = sb("on", [P, 2, OT, P])
        st = sb("st", [P, 2, OT, 6])
        dif = sb("dif", [P, OT])
        m2 = sb("m2", [P, OT])
        msum = sb("msum", [P, 2, OT])
        sq = sb("sq", [P, OT])
        sqp = sb("sqp", [P, OT])
        tot = sb("tot", [P, OT])
        std = sb("std", [P, OT])
        rstd = sb("rstd", [P, 2, OT])
        nmr = sb("nmr", [P, 2, OT])

        xt_ps = ps("xt_ps", [P, QE])
        c_ps = [ps(f"c_ps{i}", [P, QE]) for i in range(3)]
        mt_ps = ps("mt_ps", [P, QE])
        m_ps = ps("m_ps", [P, QE])
        agg_ps = ps("agg_ps", [P, OT, P])
        pro_ps = agg_ps[:, OT - 1, :]

        s_zero = sem("s_zero")
        s_cst = sem("s_cst")
        s_w = sem("s_w")
        s_wz = sem("s_wz")
        s_wsc = sem("s_wsc")
        s_tab = sem("s_tab")
        s_dstf = sem("s_dstf")
        s_iota = sem("s_iota")
        s_ha = sem("s_ha")
        s_hs = sem("s_hs")
        s_hc = sem("s_hc")
        s_hr = sem("s_hr")
        s_hl = sem("s_hl")
        s_hw = sem("s_hw")
        s_dh = sem("s_dh")
        s_q = sem("s_q")
        s_oh = sem("s_oh")
        s_hist = sem("s_hist")
        s_pre = sem("s_pre")
        s_roff = sem("s_roff")
        s_bad = sem("s_bad")
        s_badp = sem("s_badp")
        s_flag = sem("s_flag")
        s_lod = sem("s_lod")

        s_idx = sem("s_idx")
        s_xg = [sem(f"s_xg{i}") for i in range(2)]
        s_ht = [sem(f"s_ht{i}") for i in range(2)]
        s_xt = sem("s_xt")
        s_xtc = sem("s_xtc")
        s_coef = sem("s_coef")
        s_prod = sem("s_prod")
        s_mt = sem("s_mt")
        s_mtc = sem("s_mtc")
        s_m = sem("s_m")
        s_mc = sem("s_mc")
        s_ms = [sem(f"s_ms{i}") for i in range(2)]
        s_win = [sem(f"s_win{i}") for i in range(2)]
        s_xn = [sem(f"s_xn{i}") for i in range(2)]
        s_dl = sem("s_dl")
        s_mask = sem("s_mask")
        s_agg = sem("s_agg")
        s_add = sem("s_add")
        s_st = sem("s_st")
        s_sm = sem("s_sm")
        s_dif = sem("s_dif")
        s_sq = sem("s_sq")
        s_sqp = sem("s_sqp")
        s_tot = sem("s_tot")
        s_std = sem("s_std")
        s_rs = sem("s_rs")
        s_nm = sem("s_nm")
        s_norm = sem("s_norm")
        s_out = [sem(f"s_out{i}") for i in range(2)]

        s_cpy = sem("s_cpy")
        s_gtri = sem("s_gtri")
        s_gy = sem("s_gy")
        s_gm = sem("s_gm")
        s_gi = sem("s_gi")
        s_gg = sem("s_gg")
        s_gt = sem("s_gt")
        s_ge = sem("s_ge")
        s_gl = sem("s_gl")
        s_gc = sem("s_gc")
        s_gx = sem("s_gx")
        s_ga = sem("s_ga")
        s_gs = sem("s_gs")
        s_gsc = sem("s_gsc")

        block = ctx.enter_context(nc.Block())

        def prologue_sp(sp):
            sp.dma_start(cst_sb[:, :], cst[:, :]).then_inc(s_cst, 16)
            sp.dma_start(gsel_f[:, :], gsel[:, :]).then_inc(s_cst, 16)
            sp.dma_start(ha[0:90, :], attrT.rearrange("j (r c) -> (j r) c", c=AP_COLS)).then_inc(s_ha, 16)
            sp.dma_start(ha[90:100, :], attrT[6:7, :].rearrange("j (r c) -> (j r) c", c=AP_COLS)).then_inc(s_ha, 16)
            sp.wait_ge(s_zero, 1)
            sp.dma_start(dh[:, 0:DC], dst.rearrange("(p c) -> p c", c=DC)).then_inc(s_dh, 16)
            sp.dma_start(dh[0:DP - 1, DC:DC + 1], dst[DC:N_EDGES].rearrange("(p c) -> p c", c=DC)[:, 0:1], allow_slow_non_contiguous=True).then_inc(s_dh, 16)
            sp.dma_start(src_tab[:, 0:E_FULL], srcT[:, :]).then_inc(s_tab, 16)
            sp.dma_start(src_tab[0:E_TAIL, E_FULL:E_FULL + 1], src_tail[:, :]).then_inc(s_tab, 16)
            sp.dma_start(dst_tab[:, 0:E_FULL], dstT[:, :]).then_inc(s_tab, 16)
            sp.dma_start(dst_tab[0:E_TAIL, E_FULL:E_FULL + 1], dst_tail[:, :]).then_inc(s_tab, 16)
            sp.wait_ge(s_wz, 1)
            sp.dma_start(w_raw[0:MUL, 0:MUL], w0[:, 0, :]).then_inc(s_w, 16)
            sp.dma_start(w_raw[0:MUL, MUL:2 * MUL], w1[:, 0, :]).then_inc(s_w, 16)
            for i in range(3):
                sp.dma_start(w_raw[MUL + i:P:3, 0:MUL], w3[:, 0, :]).then_inc(s_w, 16)
                sp.dma_start(w_raw[MUL + i:P:3, MUL:2 * MUL], w4[:, 0, :]).then_inc(s_w, 16)
                sp.dma_start(w_raw[MUL + i:P:3, (2 + i) * MUL:(3 + i) * MUL], w2[:, 0, :]).then_inc(s_w, 16)
            for i in range(2 * PARTS):
                half = slice(i % 2 * AP_HALF, (i % 2 + 1) * AP_HALF)
                if i < 4:
                    sp.wait_ge(s_hc, i + 1)
                else:
                    sp.wait_ge(s_hl, i - 3)
                part = harm_d[i // 2 * COEF:(i // 2 + 1) * COEF, :].rearrange("j (r c) -> (j r) c", c=AP_COLS)
                sp.dma_start(part[:, half], hp[i // 2][:, half]).then_inc(s_hw, 16)
            sp.wait_ge(s_hw, 16 * 2 * PARTS)

        def windows_sp(sp):
            sp.wait_ge(s_flag, 1)
            sp.dma_start(lo_d.rearrange("a (p c) -> (a p) c", c=HB), lo_i[:, :]).then_inc(s_lod, 16)
            sp.wait_ge(s_lod, 16)
            sp.dma_start(lo_row[:, :], lo_d[:, :]).then_inc(s_lod, 16)
            sp.wait_ge(s_lod, 32)

        def prologue_pool(pool):
            g = nc.gpsimd
            g.iota(iota_f[:, :], pattern=[[1, P]], base=0, channel_multiplier=0, allow_small_or_imprecise_dtypes=True)
            g.iota(iota_b[:, :, :], pattern=[[1, HB], [0, HCH]], base=0, channel_multiplier=0,
                   allow_small_or_imprecise_dtypes=True)
            g.iota(node_base[:, :], pattern=[[P, NO * OT]], base=0, channel_multiplier=0,
                   allow_small_or_imprecise_dtypes=True)
            g.iota(bound[:, :], pattern=[[QE, HB // OT], [0, OT]], base=(STORED + 1) * QE - P,
                   channel_multiplier=QE * HB // OT, allow_small_or_imprecise_dtypes=True)
            g.memset(upper[:, :], 1.0).then_inc(s_iota, 1)
            pool.wait_ge(s_iota, 1)
            g.affine_select(out=upper[:, :], in_=upper[:, :], compare_op=ALU.is_gt, fill=0.0, base=0,
                            pattern=[[1, HB]], channel_multiplier=-1).then_inc(s_iota, 1)
            g.memset(quarter[:, :], float(P // 4)).then_inc(s_iota, 1)

        def prologue_act(act):
            for i in range(4):
                half = slice(i % 2 * AP_HALF, (i % 2 + 1) * AP_HALF)
                act.wait_ge(s_hs if i < 2 else s_hr, i % 2 + 1)
                nc.scalar.copy(hp[i // 2][:, half], ha[:, half]).then_inc(s_hc, 1)

        def prologue_dve(dve):
            v = nc.vector
            v.memset(src_tab[:, :], 0)
            v.memset(dst_tab[:, :], NO_NODE)
            v.memset(dh[:, :], NO_NODE).then_inc(s_zero, 1)
            v.memset(w_raw[:, :], 0.0).then_inc(s_wz, 1)
            v.memset(eps_sb[:, :], EPS)
            v.memset(ones_sb[:, :], 1.0)
            v.memset(badc[:, :], 0.0).then_inc(s_pre, 1)
            dve.wait_ge(s_dh, 32)
            v.tensor_scalar(qi[:, 0, :], dh[:, 0:DC], 12, None, ALU.logical_shift_right)
            v.tensor_scalar(qi[:, 1, :], dh[:, 0:DC], 7, HB - 1, ALU.logical_shift_right,
                            ALU.bitwise_and).then_inc(s_q, 1)
            dve.wait_ge(s_q, 1)
            v.tensor_copy(qb[:, :, :], qi[:, :, :]).then_inc(s_q, 1)
            dve.wait_ge(s_iota, 3)
            dve.wait_ge(s_q, 2)

            def one_hots(ch):
                need(dve, s_hist, ch - 1)
                for d in range(2):
                    last = v.tensor_tensor(
                        oh[:, ch % 2, d, :, :], iota_b[:, :, :],
                        qb[:, d, ch * HCH:(ch + 1) * HCH].unsqueeze(1).to_broadcast([DP, HB, HCH]), ALU.is_equal)
                last.then_inc(s_oh, 1)

            halves = [slice(i * AP_HALF, (i + 1) * AP_HALF) for i in range(2)]
            one_hots(0)
            one_hots(1)
            dve.wait_ge(s_cst, 32)
            dve.wait_ge(s_ha, 32)
            for half in halves:
                v.tensor_scalar(ha[:, half], ha[:, half], a_scale, None, ALU.mult).then_inc(s_hs, 1)
            dve.wait_ge(s_tab, 64)
            v.tensor_copy(dstf_tab[:, :], dst_tab[:, :]).then_inc(s_dstf, 1)
            dve.wait_ge(s_w, 16 * 11)
            v.tensor_copy(gsel_sb[:, :], gsel_f[:, :])
            v.tensor_tensor(w_sb[:, :], w_raw[:, :], w_scale, ALU.mult).then_inc(s_wsc, 1)
            for i, half in enumerate(halves):
                dve.wait_ge(s_hc, 1 + i)
                v.tensor_tensor(ha[:, half], ha[:, half], hp[0][:, half], ALU.subtract).then_inc(s_hr, 1)
            one_hots(2)
            for i, half in enumerate(halves):
                dve.wait_ge(s_hc, 3 + i)
                v.tensor_tensor(hp[2][:, half], ha[:, half], hp[1][:, half], ALU.subtract).then_inc(s_hl, 1)
            one_hots(3)

        def windows_dve(dve):
            v = nc.vector
            v.tensor_tensor(bad[:, :], dh[:, 0:DC], dh[:, 1:DC + 1], ALU.is_gt).then_inc(s_pre, 1)
            dve.wait_ge(s_pre, 2)
            v.tensor_reduce(badc[0:DP, 0:1], bad[:, :], AXX, ALU.add).then_inc(s_pre, 1)
            dve.wait_ge(s_hist, DC // HCH)
            v.tensor_copy(hist[:, :], pro_ps[0:HB, 0:HB])
            v.tensor_copy(pre[:, 0, :], pro_ps[0:HB, 0:HB])
            v.tensor_reduce(rowsum[:, :], pro_ps[0:HB, 0:HB], AXX, ALU.add).then_inc(s_pre, 1)
            dve.wait_ge(s_pre, 4)
            a, step, n = 0, 1, 4
            while step < HB:
                v.tensor_copy(pre[:, 1 - a, 0:step], pre[:, a, 0:step])
                v.tensor_tensor(pre[:, 1 - a, step:HB], pre[:, a, step:HB], pre[:, a, 0:HB - step],
                                ALU.add).then_inc(s_pre, 1)
                a, step, n = 1 - a, 2 * step, n + 1
                dve.wait_ge(s_pre, n)
            v.tensor_tensor(lo_f[:, :], pre[:, a, :], hist[:, :], ALU.subtract).then_inc(s_pre, 1)
            dve.wait_ge(s_roff, 1)
            v.tensor_copy(roff[:, :], pro_ps[0:HB, 64:65]).then_inc(s_pre, 1)
            dve.wait_ge(s_pre, n + 2)
            v.tensor_scalar(lo_f[:, :], lo_f[:, :], roff[:, 0:1], None, ALU.add).then_inc(s_pre, 1)
            dve.wait_ge(s_pre, n + 3)
            v.tensor_copy(lo_i[:, :], lo_f[:, :])
            v.tensor_scalar(bad2[:, 0, :], hist[:, :], float(P), None, ALU.is_gt)
            v.tensor_tensor(bad2[:, 1, :], lo_f[:, :], bound[:, :], ALU.is_gt).then_inc(s_pre, 1)
            dve.wait_ge(s_pre, n + 4)
            v.tensor_reduce(badc[0:HB, 1:2], bad2[:, :, :].rearrange("p a b -> p (a b)"), AXX,
                            ALU.add).then_inc(s_bad, 1)
            dve.wait_ge(s_badp, 1)
            v.tensor_scalar(flag[:, :], pro_ps[0:1, 96:97], float(FORCE), None, ALU.add).then_inc(s_flag, 1)

        def prologue_pe(pe):
            for ch in range(DC // HCH):
                pe.wait_ge(s_oh, ch + 1)
                for c in range(HCH):
                    last = nc.tensor.matmul(pro_ps[0:HB, 0:HB], oh[:, ch % 2, 0, :, c], oh[:, ch % 2, 1, :, c],
                                            start=(ch == 0 and c == 0), stop=(ch == DC // HCH - 1 and c == HCH - 1))
                last.then_inc(s_hist, 1)

        def windows_pe(pe):
            pe.wait_ge(s_pre, 4)
            nc.tensor.matmul(pro_ps[0:HB, 64:65], upper[:, :], rowsum[:, :], start=True, stop=True).then_inc(s_roff, 1)
            pe.wait_ge(s_bad, 1)
            nc.tensor.matmul(pro_ps[0:1, 96:97], badc[:, 0:1], ones_sb[:, :], start=True, stop=False)
            nc.tensor.matmul(pro_ps[0:1, 96:97], badc[:, 1:2], ones_sb[:, :], start=False, stop=True).then_inc(s_badp, 1)

        def exists(at, off, n):
            return 0 <= at + off < n

        def side(s, off=0):
            return (s + off) % 2

        def pool_gather(pool, q0, s):
            first = fixed(pool, (q0 + s) * QT)
            free, made = count(pool, q0 + s - 1), count(pool, q0 + s + 1)
            h = side(s)
            pool.wait_ge(s_tab, 64)
            need(pool, s_xt, free)
            nc.gpsimd.tensor_copy(idx[:, h, :], src_tab[:, bass.ds(first, QT)]).then_inc(s_idx, 1)
            pool.wait_ge(s_tab, 64)
            pool.wait_ge(s_idx, made)
            for t in range(QT):
                pool.indirect_dma_start(
                    out=xg[:, h, t, :], out_offset=None, in_=x[:, :],
                    in_offset=bass.IndirectOffsetOnAxis(ap=idx[:, h, t:t + 1], axis=0),
                    bounds_check=N_NODES - 1, oob_is_err=False).then_inc(s_xg[h], 16)

        def pool_slot(pool, q0, s, at, nodes):
            q = q0 + s
            o = q - LAG
            if nodes and exists(at, s - LAG - 1, NO):
                ln_var(pool, side(s, -LAG - 1), o - 1)
            if nodes and exists(at, s - LAG + 1, NO):
                h = side(s, 1 - LAG)
                need(pool, s_mask, o)
                pool.wait_ge(s_win[h], turns(q0, s - LAG + 1, 16 * OT))
                nc.gpsimd.tensor_tensor(dloc[:, h, :], win[:, h, :, P], node_base[:, bass.ds((o + 1) * OT, OT)],
                                        ALU.subtract).then_inc(s_dl, 1)
            if exists(at, s + 2, NQ):
                pool_gather(pool, q0, s + 2)

        def pe_transpose(pe, q0, s):
            h = side(s)
            pe.wait_ge(s_xg[h], turns(q0, s, 16 * QT))
            need(pe, s_xtc, q0 + s)
            for t in range(QT):
                last = nc.tensor.transpose(xt_ps[:, t * P:(t + 1) * P], xg[:, h, t, :], ident)
            last.then_inc(s_xt, 1)

        def pe_coef(pe, q0, s, blocks):
            for c in blocks:
                h = side(s)
                if c == 0:
                    pe.wait_ge(s_ht[h], turns(q0, s, 16))
                need(pe, s_prod, 5 * (q0 + s) + (-1, 0, -2, 1, 2)[c])
                nc.tensor.matmul(c_ps[c % 3][:, :], gsel_sb[:, c * P:(c + 1) * P], ht[:, h, :],
                                 start=True, stop=True).then_inc(s_coef, 1)

        def pe_slot(pe, q0, s, at, nodes):
            q = q0 + s
            o = q - LAG
            h = side(s)
            if at + s == 0:
                pe_transpose(pe, 0, 0)
                pe_coef(pe, 0, 0, range(0, 3))
            node = nodes and exists(at, s - LAG, NO)
            if node:
                pe.wait_ge(s_mask, o + 1)
                need(pe, s_add, o)
            for j in range(OT):
                if j in (2, 4) and exists(at, s, NQ):
                    pe_coef(pe, q0, s, (2 + j // 2,))
                if node:
                    last = nc.tensor.matmul(agg_ps[:, j, :], mask[:, side(s, -LAG), j, :],
                                            win[:, side(s, -LAG), j, 0:P], start=True, stop=True)
            if node:
                last.then_inc(s_agg, 1)
            if exists(at, s + 1, NQ):
                pe_transpose(pe, q0, s + 1)
            if exists(at, s, NQ):
                pe.wait_ge(s_prod, 5 * q + 5)
                need(pe, s_mtc, q)
                for c in range(4):
                    wc = w_sb[:, 0:MUL] if c == 0 else w_sb[:, MUL:2 * MUL]
                    nc.tensor.matmul(mt_ps[c * MUL:(c + 1) * MUL, :], wc, prod[:, h, c, :], start=True, stop=(c == 0),
                                     tile_position=(0, c * MUL))
                for c in range(1, 4):
                    last = nc.tensor.matmul(mt_ps[c * MUL:(c + 1) * MUL, :], w_sb[:, (1 + c) * MUL:(2 + c) * MUL],
                                            prod[:, h, 4, :], start=False, stop=True, tile_position=(0, c * MUL))
                last.then_inc(s_mt, 1)
            if exists(at, s + 1, NQ):
                pe_coef(pe, q0, s + 1, range(0, 3))
            if exists(at, s, NQ):
                pe.wait_ge(s_mtc, q + 1)
                need(pe, s_mc, q)
                for t in range(QT):
                    last = nc.tensor.transpose(m_ps[:, t * P:(t + 1) * P], mts[:, t * P:(t + 1) * P], perm)
                last.then_inc(s_m, 1)

        def ln_stats(dve, yt, sl):
            for j in range(OT):
                last = nc.vector.bn_stats(st[:, sl, j, :], yt[:, j, :])
            last.then_inc(s_st, 1)

        def ln_var(pool, sl, n):
            g = nc.gpsimd
            need(pool, s_std, n)
            pool.wait_ge(s_st, n + 1)
            g.tensor_tensor(dif[:, :], st[:, sl, :, 1], st[:, sl, :, 4], ALU.subtract).then_inc(s_dif, 1)
            g.tensor_tensor(m2[:, :], st[:, sl, :, 2], st[:, sl, :, 5], ALU.add)
            g.tensor_tensor(msum[:, sl, :], st[:, sl, :, 1], st[:, sl, :, 4], ALU.add).then_inc(s_sm, 1)
            pool.wait_ge(s_dif, n + 1)
            g.tensor_tensor(sq[:, :], dif[:, :], dif[:, :], ALU.mult).then_inc(s_sq, 1)
            pool.wait_ge(s_sq, n + 1)
            g.tensor_tensor(sqp[:, :], sq[:, :], quarter[:, :], ALU.mult).then_inc(s_sqp, 1)
            pool.wait_ge(s_sm, n + 1)
            pool.wait_ge(s_sqp, n + 1)
            g.tensor_tensor(tot[:, :], m2[:, :], sqp[:, :], ALU.add).then_inc(s_tot, 1)

        def ln_scale(dve, sl, n):
            dve.wait_ge(s_std, n + 1)
            nc.vector.reciprocal(rstd[:, sl, :], std[:, :]).then_inc(s_rs, 1)

        def ln_shift(dve, sl, n):
            dve.wait_ge(s_sm, n + 1)
            dve.wait_ge(s_rs, n + 1)
            nc.vector.scalar_tensor_tensor(nmr[:, sl, :], msum[:, sl, :], -0.5, rstd[:, sl, :],
                                           ALU.mult, ALU.mult).then_inc(s_nm, 1)

        def ln_std(act, n):
            act.wait_ge(s_tot, n + 1)
            nc.scalar.activation(std[:, :], tot[:, :], ACT.Sqrt, bias=eps_sb[:, :], scale=1.0 / P).then_inc(s_std, 1)

        def ln_apply(ot, yt, sl, tiles):
            for j in tiles:
                last = nc.scalar.activation(ot[:, j, :], yt[:, j, :], ACT.Identity, bias=nmr[:, sl, j:j + 1],
                                            scale=rstd[:, sl, j:j + 1])
            return last

        def dve_slot(dve, q0, s, at, nodes):
            q = q0 + s
            o = q - LAG
            v = nc.vector
            h, ho, hp_ = side(s), side(s, -LAG), side(s, -LAG - 1)
            before = nodes and exists(at, s - LAG - 1, NO)
            for c in range(TERMS):
                if exists(at, s, NQ):
                    if c == 0:
                        dve.wait_ge(s_xtc, q + 1)
                        need(dve, s_mt, q - 1)
                    dve.wait_ge(s_coef, 5 * q + c + 1)
                    v.tensor_tensor(prod[:, h, c, :], xts[:, h, :], c_ps[c % 3][:, :], ALU.mult).then_inc(s_prod, 1)
                if before and c == 3:
                    ln_scale(dve, hp_, o - 1)
                if before and c == 4:
                    ln_shift(dve, hp_, o - 1)
            if nodes and exists(at, s - LAG + 1, NO):
                hn = side(s, 1 - LAG)
                need(dve, s_agg, o)
                dve.wait_ge(s_dl, o + 2)
                v.tensor_tensor(mask[:, hn, :, :], iota_f[:, :].unsqueeze(1).to_broadcast([P, OT, P]),
                                dloc[:, hn, :].unsqueeze(2).to_broadcast([P, OT, P]), ALU.is_equal).then_inc(s_mask, 1)
            if nodes and exists(at, s - LAG, NO):
                dve.wait_ge(s_xn[ho], turns(q0, s - LAG, 16) + (16 if at + s - LAG == NO - 1 else 0))
                need(dve, s_norm, o - 1)
                dve.wait_ge(s_agg, o + 1)
                v.tensor_tensor(y[:, ho, :, :], xn[:, ho, :, :], agg_ps[:, :, :], ALU.add).then_inc(s_add, 1)
                dve.wait_ge(s_add, o + 1)
                ln_stats(dve, y[:, ho, :, :], ho)

        def oct_io(eng, first, last, dram, load, buf, done):
            def move(rows, tile):
                eng.dma_start(*((tile, rows) if load else (rows, tile))).then_inc(done, 16)
            if not last:
                move(dram[bass.ds(first, OT * P), :].rearrange("(j p) d -> p j d", p=P), buf[:, :, :])
                return
            first = (NO - 1) * OT * P
            full = (N_NODES - first) // P
            rest = N_NODES - first - full * P
            move(dram[first:first + full * P, :].rearrange("(j p) d -> p j d", p=P), buf[:, 0:full, :])
            move(dram[first + full * P:N_NODES, :], buf[0:rest, full, :])

        def act_transposed(act, q0, s):
            need(act, s_prod, 5 * (q0 + s - 1))
            act.wait_ge(s_xt, q0 + s + 1)
            nc.scalar.copy(xts[:, side(s), :], xt_ps[:, :]).then_inc(s_xtc, 1)

        def act_slot(act, q0, s, at, nodes):
            q = q0 + s
            o = q - LAG
            h, hp_, hs = side(s), side(s, -LAG - 1), side(s, -LAG - 2)
            msg = exists(at, s, NQ)
            before = nodes and exists(at, s - LAG - 1, NO)
            if at + s == 0:
                act_transposed(act, 0, 0)
            if before:
                ln_std(act, o - 1)
            if exists(at, s - 1, NQ):
                rows = fixed(act, (q - 1) * QE)
                act.wait_ge(s_mc, q)
                act.dma_start(msg_d[bass.ds(rows, QE), :].rearrange("(t p) d -> p t d", p=P),
                             mrow[:, 1 - h, :, :]).then_inc(s_ms[1 - h], 16)
            if nodes and exists(at, s - LAG - 2, NO):
                rows = fixed(act, (o - 2) * OT * P)
                act.wait_ge(s_norm, o - 1)
                oct_io(act, rows, at + s - LAG - 2 == NO - 1, out, False, on[:, hs, :, :], s_out[hs])
            if exists(at, s + 1, NQ):
                act_transposed(act, q0, s + 1)
            if before:
                need(act, s_out[hp_], turns(q0, s - LAG - 3, 16))
                act.wait_ge(s_nm, o)
                ln_apply(on[:, hp_, :, :], y[:, hp_, :, :], hp_, range(0, OT // 2))
            if msg:
                need(act, s_m, q)
                act.wait_ge(s_mt, q + 1)
                nc.scalar.copy(mts[:, :], mt_ps[:, :]).then_inc(s_mtc, 1)
            if before:
                ln_apply(on[:, hp_, :, :], y[:, hp_, :, :], hp_, range(OT // 2, OT)).then_inc(s_norm, 1)
            if msg:
                act.wait_ge(s_m, q + 1)
                need(act, s_ms[h], turns(q0, s - 2, 16))
                act.wait_ge(s_dstf, 1)
                nc.scalar.copy(mrow[:, h, :, P], dstf_tab[:, bass.ds(q * QT, QT)])
                nc.scalar.copy(mrow[:, h, :, 0:P], m_ps[:, :].rearrange("p (t f) -> p t f", f=P)).then_inc(s_mc, 1)

        def sp_slot(sp, q0, s, at, nodes):
            q = q0 + s
            o = q - LAG
            h, hn = side(s), side(s, 2 - LAG)
            if nodes and exists(at, s - LAG + 2, NO):
                _, los = nc.values_load_multi_w_load_instructions(
                    lo_row[0:1, bass.ds((o + 2) * OT, OT)], engines=[mybir.EngineType.SP], min_val=0,
                    max_val=N_EDGES, skip_runtime_bounds_check_because="a sum of a histogram of N_EDGES edges")
                rows = fixed(sp, (o + 2) * OT * P)
                stored = count(sp, turns(q0, s - 2, 16)) if exists(at, s - 2, NQ) else 16 * (NQ // 2)
                stored2 = count(sp, turns(q0, s - 3, 16)) if exists(at, s - 3, NQ) else 16 * (NQ // 2)
                free = count(sp, o + 1)
                sp.wait_ge(s_ms[h], stored)
                sp.wait_ge(s_ms[1 - h], stored2)
                need(sp, s_agg, free)
                for j in range(OT):
                    sp.dma_start(win[:, hn, j, :], msg_d[bass.ds(los[j], P), :]).then_inc(s_win[hn], 16)
                need(sp, s_add, free)
                oct_io(sp, rows, at + s - LAG + 2 == NO - 1, x, True, xn[:, hn, :, :], s_xn[hn])
            if exists(at, s + 2, NQ):
                cols = fixed(sp, (q + 2) * QE)
                sp.wait_ge(s_coef, 5 * q + 5)
                if at + s + 2 < NQ - 1:
                    sp.dma_start(ht[:, h, :], harm_d[:, bass.ds(cols, QE)]).then_inc(s_ht[h], 16)
                else:
                    sp.dma_start(ht[:, h, 0:N_EDGES - cols], harm_d[:, cols:N_EDGES]).then_inc(s_ht[h], 16)

        SHARED = LAG - 2

        def straight(eng, slot, nodes, first, end):
            for q in range(first, end):
                slot(eng, q - q % 2, q % 2, q - q % 2, nodes)

        def run(eng, slot, nodes):
            lead, tail = LAG + 3, NQ - 4
            straight(eng, slot, nodes, SHARED, lead)
            with eng.Fori(lead, tail - 1, 2) as q0:
                for s in range(2):
                    slot(eng, q0, s, lead, nodes)
            straight(eng, slot, nodes, tail, NQ + (LAG + 2 if nodes else 1))

        NT = E_PAD // P
        edge_m = win[:, 0, 0, 0:P]
        edge_d = win[:, 0, 0, P:P + 1]
        d_wide, same, earlier, below = (mask[:, 0, i, :] for i in range(4))
        rows_y = xn[:, 0, 0, :]
        CP = 125

        def general_sp(sp):
            sp.dma_start(out.rearrange("(a b) d -> a (b d)", b=CP), x.rearrange("(a b) d -> a (b d)", b=CP)).then_inc(s_cpy, 16)
            sp.wait_ge(s_ms[0], 16 * (NQ // 2))
            sp.wait_ge(s_ms[1], 16 * (NQ // 2))

            def load(t, last):
                rows = fixed(sp, t * P)
                need(sp, s_gsc, last)
                sp.dma_start(win[:, 0, 0, :], msg_d[bass.ds(rows, P), :]).then_inc(s_gm, 16)
            load(0, 0)
            with sp.Fori(1, NT) as t:
                load(t, count(sp, t * 16))

            def normalise(o, is_last):
                rows, stored, n = fixed(sp, o * OT * P), count(sp, o * 16), count(sp, o + 1)
                need(sp, s_out[0], stored)
                oct_io(sp, rows, is_last, out, True, y[:, 0, :, :], s_xn[0])
                sp.wait_ge(s_norm, n)
                oct_io(sp, rows, is_last, out, False, on[:, 0, :, :], s_out[0])
            sp.wait_ge(s_gsc, 16 * NT)
            normalise(0, False)
            with sp.Fori(1, NO - 1) as o:
                normalise(o, False)
            normalise(NO - 1, True)
            sp.wait_ge(s_out[0], 16 * (NO + 1))

        def general_pool(pool):
            nc.gpsimd.memset(below, 1.0).then_inc(s_gtri, 1)
            pool.wait_ge(s_gtri, 1)
            nc.gpsimd.affine_select(out=below, in_=below, compare_op=ALU.is_gt, fill=0.0, base=0,
                                    pattern=[[-1, P]], channel_multiplier=1).then_inc(s_gtri, 1)
            pool.wait_ge(s_cpy, 16)
            with pool.Fori(0, NT) as t:
                n = count(pool, t + 1)
                pool.wait_ge(s_gy, 1)
                pool.wait_ge(s_gi, n)
                pool.indirect_dma_start(out=rows_y, out_offset=None, in_=out[:, :],
                                        in_offset=bass.IndirectOffsetOnAxis(ap=idx[:, 0, 0:1], axis=0),
                                        bounds_check=N_NODES - 1, oob_is_err=False).then_inc(s_gg, 16)
                pool.wait_ge(s_gy, 1)
                pool.wait_ge(s_gx, n)
                pool.wait_ge(s_gs, n)
                pool.indirect_dma_start(out=out[:, :], out_offset=bass.IndirectOffsetOnAxis(ap=idx[:, 1, 0:1], axis=0),
                                        in_=rows_y, in_offset=None,
                                        bounds_check=N_NODES - 1, oob_is_err=False).then_inc(s_gsc, 16)
                pool.wait_ge(s_gsc, t * 16 + 16)
            ln_var(pool, 0, 0)
            with pool.Fori(1, NO) as o:
                ln_var(pool, 0, o)

        def general_pe(pe):
            with pe.Fori(0, NT) as t:
                pe.wait_ge(s_gi, t + 1)
                nc.tensor.transpose(pro_ps[:, :], d_wide, ident).then_inc(s_gt, 1)
                pe.wait_ge(s_ge, t + 1)
                nc.tensor.matmul(agg_ps[:, 0, :], same, edge_m, start=True, stop=True).then_inc(s_ga, 1)

        def general_dve(dve):
            v = nc.vector
            v.memset(rows_y, 0.0).then_inc(s_gy, 1)
            dve.wait_ge(s_gtri, 2)
            with dve.Fori(0, NT) as t:
                dve.wait_ge(s_gm, t * 16 + 16)
                v.tensor_copy(idx[:, 0, 0:1], edge_d)
                v.tensor_copy(d_wide, edge_d.to_broadcast([P, P])).then_inc(s_gi, 1)
                dve.wait_ge(s_gi, t + 1)
                dve.wait_ge(s_gt, t + 1)
                v.tensor_tensor(same, pro_ps[:, :], d_wide, ALU.is_equal).then_inc(s_ge, 1)
                dve.wait_ge(s_ge, t + 1)
                v.tensor_tensor(earlier, same, below, ALU.mult).then_inc(s_gl, 1)
                dve.wait_ge(s_gl, t + 1)
                v.tensor_reduce(dloc[:, 0, 0:1], earlier, AXX, ALU.add).then_inc(s_gc, 1)
                dve.wait_ge(s_gc, t + 1)
                v.scalar_tensor_tensor(idx[:, 1, 0:1], dloc[:, 0, 0:1], float(1 << 17), edge_d, ALU.mult,
                                       ALU.add).then_inc(s_gx, 1)
                dve.wait_ge(s_gg, t * 16 + 16)
                dve.wait_ge(s_ga, t + 1)
                v.tensor_tensor(rows_y, rows_y, agg_ps[:, 0, :], ALU.add).then_inc(s_gs, 1)

            def normalise(o):
                ln_stats(dve, y[:, 0, :, :], 0)
                ln_scale(dve, 0, o)
                ln_shift(dve, 0, o)
            with dve.Fori(0, NO - 1) as o:
                dve.wait_ge(s_xn[0], o * 16 + 16)
                normalise(o)
            dve.wait_ge(s_xn[0], 16 * (NO + 1))
            normalise(NO - 1)

        def general_act(act):
            with act.Fori(0, NO) as o:
                ln_std(act, o)
                act.wait_ge(s_nm, o + 1)
                ln_apply(on[:, 0, :, :], y[:, 0, :, :], 0, range(OT)).then_inc(s_norm, 1)

        def ways(eng, fast, slow):
            eng.wait_ge(s_flag, 1)
            f = eng.value_load(flag[0:1, 0:1], min_val=0, max_val=1 << 20)
            with eng.If(f == 0):
                fast()
            with eng.Else():
                slow()

        @block.sync
        def _(sp):
            prologue_sp(sp)
            for h in range(2):
                sp.dma_start(ht[:, h, :], harm_d[:, h * QE:(h + 1) * QE]).then_inc(s_ht[h], 16)
            straight(sp, sp_slot, False, 0, SHARED)
            windows_sp(sp)

            def fast():
                run(sp, sp_slot, True)
                sp.wait_ge(s_out[0], 16 * (NO // 2))
                sp.wait_ge(s_out[1], 16 * (NO // 2) + 16)

            def slow():
                run(sp, sp_slot, False)
                general_sp(sp)
            ways(sp, fast, slow)

        @block.gpsimd
        def _(pool):
            prologue_pool(pool)
            for s in range(2):
                pool_gather(pool, 0, s)
            straight(pool, pool_slot, False, 0, SHARED)

            def slow():
                run(pool, pool_slot, False)
                general_pool(pool)
            ways(pool, lambda: run(pool, pool_slot, True), slow)

        @block.scalar
        def _(act):
            prologue_act(act)
            straight(act, act_slot, False, 0, SHARED)

            def slow():
                run(act, act_slot, False)
                general_act(act)
            ways(act, lambda: run(act, act_slot, True), slow)

        @block.vector
        def _(dve):
            prologue_dve(dve)
            straight(dve, dve_slot, False, 0, 1)
            windows_dve(dve)
            straight(dve, dve_slot, False, 1, SHARED)

            def slow():
                run(dve, dve_slot, False)
                general_dve(dve)
            ways(dve, lambda: run(dve, dve_slot, True), slow)

        @block.tensor
        def _(pe):
            prologue_pe(pe)
            pe.wait_ge(s_cst, 32)
            pe.wait_ge(s_wsc, 1)
            straight(pe, pe_slot, False, 0, 1)
            windows_pe(pe)
            straight(pe, pe_slot, False, 1, SHARED)

            def slow():
                run(pe, pe_slot, False)
                general_pe(pe)
            ways(pe, lambda: run(pe, pe_slot, True), slow)


def wigner_3j(l1, l2, l3):
    import numpy as np
    from math import factorial

    def coeff(j1, m1, j2, m2, j3, m3):
        if m3 != m1 + m2:
            return 0.0
        vmin = int(max(-j1 + j2 + m3, -j1 + m1, 0))
        vmax = int(min(j2 + j3 + m1, j3 - j1 + j2, j3 + m3))
        f = factorial
        c = ((2.0 * j3 + 1.0) * (f(j3 + j1 - j2) * f(j3 - j1 + j2) * f(j1 + j2 - j3) * f(j3 + m3) * f(j3 - m3))
             / (f(j1 + j2 + j3 + 1) * f(j1 - m1) * f(j1 + m1) * f(j2 - m2) * f(j2 + m2))) ** 0.5
        s = 0
        for v in range(vmin, vmax + 1):
            s += ((-1) ** (v + j2 + m2) * (f(j2 + j3 + m1 - v) * f(j1 - m1 + v))
                  / (f(v) * f(j3 - j1 + j2 - v) * f(j3 + m3 - v) * f(v + j1 - j2 - m3)))
        return float(c * s)

    def basis(l):
        q = np.zeros((2 * l + 1, 2 * l + 1), dtype=np.complex128)
        for m in range(-l, 0):
            q[l + m, l + abs(m)] = 1 / np.sqrt(2)
            q[l + m, l - abs(m)] = -1j / np.sqrt(2)
        q[l, l] = 1
        for m in range(1, l + 1):
            q[l + m, l + abs(m)] = (-1) ** m / np.sqrt(2)
            q[l + m, l - abs(m)] = 1j * (-1) ** m / np.sqrt(2)
        return (-1j) ** l * q

    c = np.zeros((2 * l1 + 1, 2 * l2 + 1, 2 * l3 + 1))
    for m1 in range(-l1, l1 + 1):
        for m2 in range(-l2, l2 + 1):
            if abs(m1 + m2) <= l3:
                c[l1 + m1, l2 + m2, l3 + m1 + m2] = coeff(l1, m1, l2, m2, l3, m1 + m2)
    cc = np.einsum("ij,kl,mn,ikn->jlm", basis(l1), basis(l2), np.conj(basis(l3).T), c.astype(np.complex128))
    cr = np.real(cc)
    return cr / np.linalg.norm(cr)


def constants():
    import numpy as np
    neighbors = 10.0
    norm = {0: np.sqrt(1 / (2 * MUL)) / np.sqrt(neighbors), 1: np.sqrt(3 / (3 * MUL)) / np.sqrt(neighbors)}
    w000, w011, w101, w110, w121 = (wigner_3j(*l) for l in ((0, 0, 0), (0, 1, 1), (1, 0, 1), (1, 1, 0), (1, 2, 1)))
    t = np.abs(w121[0, 0, :]).max() or np.abs(w121[0, 1, :]).max()
    w_scale = np.zeros((P, 5 * MUL))
    g = np.zeros((COEF, TERMS, P))
    V = [slice(MUL + i, P, 3) for i in range(3)]
    w_scale[:MUL, :MUL] = norm[0] * w000[0, 0, 0]
    g[0, 0, :MUL] = 1
    w_scale[MUL:, :MUL] = norm[0] * w110[0, 0, 0]
    w_scale[:MUL, MUL:2 * MUL] = norm[1] * w011[0, 0, 0]
    w_scale[MUL:, MUL:2 * MUL] = norm[1] * t
    w_scale[MUL:, 2 * MUL:] = norm[1] * w101[0, 0, 0]
    g[0, 4, MUL:] = 1
    for i in range(3):
        for j in range(3):
            g[1 + j, 0, V[i]] = w110[i, j, 0] / w110[0, 0, 0]
        for k in range(3):
            g[1 + i, 1 + k, :MUL] = w011[0, i, k] / w011[0, 0, 0]
            for j in range(5):
                row, by = (9, np.sqrt(3)) if j == 2 else (4 + j, 1)
                g[row, 1 + k, V[i]] = w121[i, j, k] / t * by
    whole = np.rint(g)
    assert np.abs(g - whole).max() < 1e-9 and np.abs(whole).max() <= 2
    gsel = np.tile(whole.reshape(COEF, TERMS * P), (PARTS, 1)).astype(np.float32)
    ident = np.eye(P)
    perm = np.zeros((P, P))
    perm[np.arange(MUL), np.arange(MUL)] = 1
    for k in range(3):
        for w in range(MUL):
            perm[MUL + k * MUL + w, MUL + 3 * w + k] = 1
    a_scale = np.ones((P, 1))
    a_scale[90:AP_ROWS] = 1 / np.sqrt(3)
    cst = np.concatenate([ident, perm, w_scale, a_scale], axis=1).astype(np.float32)
    return cst, gsel


def host_layout(inputs):
    import numpy as np
    x, src, dst, attr = (np.asarray(inputs[n]) for n in ("x", "src", "dst", "edge_attr_9"))
    full = E_FULL * P
    cst, gsel = constants()
    arrays = {
        "x": x,
        "srcT": src[:full].reshape(E_FULL, P).T, "src_tail": src[full:].reshape(E_TAIL, 1),
        "dst": dst,
        "dstT": dst[:full].reshape(E_FULL, P).T, "dst_tail": dst[full:].reshape(E_TAIL, 1),
        "attrT": attr.T,
        **{f"w{i}": np.asarray(inputs[f"L0_gnn_w{i}"]) for i in range(5)},
        "cst": cst, "gsel": gsel,
    }
    return {n: np.ascontiguousarray(a) for n, a in arrays.items()}


def kernel(**inputs):
    import numpy as _np
    import concourse.bacc as _bacc
    from concourse import mybir as _mybir
    from concourse.bass_utils import run_bass_kernel_spmd as _run

    nc = _bacc.Bacc("TRN2", target_bir_lowering=False, num_devices=1)
    arrays = host_layout(inputs)
    args = [nc.dram_tensor(n, a.shape, _mybir.dt.from_np(a.dtype), kind="ExternalInput").ap()
            for n, a in arrays.items()]
    args.append(nc.dram_tensor("out", (N_NODES, P), _mybir.dt.float32, kind="ExternalOutput").ap())
    build(nc, *args)
    r = _run(nc, [arrays], core_ids=[0])
    return r.results[0]["out"]
```

```python
import concourse.bass as bass
from concourse import mybir
from contextlib import ExitStack

FP32 = mybir.dt.float32
BF16 = mybir.dt.bfloat16
I32 = mybir.dt.int32
ALU = mybir.AluOpType
ACT = mybir.ActivationFunctionType
AXX = mybir.AxisListType.X

P = 128
N_NODES, N_EDGES = 100000, 50000
MUL = 32
QT = 4
QE = QT * P
NQ = 98
E_PAD = NQ * QE
E_FULL = N_EDGES // P
E_TAIL = N_EDGES - E_FULL * P
OT = 8
NO = 98
LAG = 7
WINS = 4
PE_TILES = 7
STORED = 1
ROW = P + 1
TERMS = 5
COEF = 10
PARTS = 3
AP_ROWS, AP_COLS = 100, 5000
PIECES = (slice(0, 4 * QE), slice(4 * QE, AP_COLS))
DP, DC = 125, 400
HCH = 100
HB = 32
NO_NODE = 1 << 22
EPS = 1e-5


def need(eng, sem, value):
    if isinstance(value, int) and value <= 0:
        return
    eng.wait_ge(sem, value)


def fixed(eng, value):
    return value if isinstance(value, int) else eng.snap(value)


def count(eng, value):
    return value if isinstance(value, int) else eng.to_reg(value)


def turns(q0, off, per, n=2):
    return q0 * (per // n) + per * (off // n + 1)


def build(nc, x, srcT, src_tail, dst, dstT, dst_tail, attrT, w0, w1, w2, w3, w4, cst, gsel, out, FORCE=0):
    ctx = ExitStack()
    with ctx:
        def sb(name, shape, dt=FP32):
            return ctx.enter_context(nc.sbuf_tensor(name, shape, dt))

        def ps(name, shape, dt=FP32):
            return ctx.enter_context(nc.psum_tensor(name, shape, dt))

        def sem(name):
            return ctx.enter_context(nc.semaphore(name))

        msg_d = nc.dram_tensor("msg_scratch", [P + E_PAD, ROW], FP32, kind="Internal").ap()
        harm_d = nc.dram_tensor("harm_scratch", [PARTS * COEF, N_EDGES], BF16, kind="Internal").ap()
        lo_d = nc.dram_tensor("lo_scratch", [1, HB * HB // 2], I32, kind="Internal").ap()

        cst_sb = sb("cst_sb", [P, 2 * P + 5 * MUL + 1])
        ident = cst_sb[:, 0:P]
        perm = cst_sb[:, P:2 * P]
        w_scale = cst_sb[:, 2 * P:2 * P + 5 * MUL]
        a_scale = cst_sb[0:AP_ROWS, 2 * P + 5 * MUL:2 * P + 5 * MUL + 1]
        gsel_f = sb("gsel_f", [PARTS * COEF, TERMS * P])
        gsel_sb = sb("gsel_sb", [PARTS * COEF, TERMS * P], BF16)
        w_raw = sb("w_raw", [P, 5 * MUL])
        w_sb = sb("w_sb", [P, 5 * MUL])
        src_tab = sb("src_tab", [P, NQ * QT], I32)
        dst_tab = sb("dst_tab", [P, NQ * QT], I32)
        dstf_tab = sb("dstf_tab", [P, NQ * QT])
        node_base = sb("node_base", [P, NO * OT])
        iota_f = sb("iota_f", [P, P])
        eps_sb = sb("eps_sb", [P, 1])
        quarter = sb("quarter", [P, OT])
        ones_sb = sb("ones_sb", [P, 1])

        ha_y = sb("ha_y", [P, AP_COLS])
        ha = ha_y[0:AP_ROWS, :]
        hp = [sb(f"hp{i}", [AP_ROWS, AP_COLS], BF16) for i in range(PARTS)]
        dh = sb("dh", [DP, DC + 1], I32)
        qi = sb("qi", [DP, 2, DC], I32)
        qb = sb("qb", [DP, 2, DC], BF16)
        iota_b = sb("iota_b", [DP, HB, HCH], BF16)
        oh = sb("oh", [DP, 2, 2, HB, HCH], BF16)
        hist = sb("hist", [HB, HB])
        pre = sb("pre", [HB, 2, HB])
        rowsum = sb("rowsum", [HB, 1])
        roff = sb("roff", [HB, 1])
        upper = sb("upper", [HB, HB])
        lo_f = sb("lo_f", [HB, HB])
        lo_i = sb("lo_i", [HB, HB // 2], I32)
        bound = sb("bound", [HB, HB])
        bad = sb("bad", [DP, DC])
        bad2 = sb("bad2", [HB, 2, HB])
        badc = sb("badc", [P, 2])
        flag = sb("flag", [1, 1], I32)
        lo_row = sb("lo_row", [1, HB * HB // 2], I32)

        idx = sb("idx", [P, WINS, QT], I32)
        xg = sb("xg", [P, WINS, QT, P])
        ht = sb("ht", [PARTS * COEF, WINS * QE], BF16)
        xts = sb("xts", [P, 2, QE])
        prod = sb("prod", [P, 2, TERMS, QE])
        mts = sb("mts", [P, QE])
        mrow = sb("mrow", [P, 2, QT, ROW])
        win = sb("win", [P, WINS, OT, ROW])
        dloc = sb("dloc", [P, 2, OT])
        mask = sb("mask", [P, 2, OT, P])
        xn = sb("xn", [P, WINS * OT, P])
        y = ha_y[:, 0:WINS * OT * P].rearrange("p (w j f) -> p w j f", w=WINS, j=OT)
        on = sb("on", [P, WINS, OT, P])
        st = sb("st", [P, 2, OT, 6])
        dif = sb("dif", [P, OT])
        m2 = sb("m2", [P, OT])
        msum = sb("msum", [P, 2, OT])
        sq = sb("sq", [P, OT])
        sqp = sb("sqp", [P, OT])
        tot = sb("tot", [P, OT])
        std = sb("std", [P, OT])
        rstd = sb("rstd", [P, 2, OT])
        nmr = sb("nmr", [P, 2, OT])

        xt_ps = ps("xt_ps", [P, QE])
        c_ps = [ps(f"c_ps{i}", [P, QE]) for i in range(3)]
        mt_ps = ps("mt_ps", [P, QE])
        m_ps = ps("m_ps", [P, QE])
        agg_ps = ps("agg_ps", [P, OT, P])
        pro_ps = agg_ps[:, OT - 1, :]

        s_zero = sem("s_zero")
        s_cst = sem("s_cst")
        s_gsel = sem("s_gsel")
        s_w = sem("s_w")
        s_wz = sem("s_wz")
        s_wsc = sem("s_wsc")
        s_tab = sem("s_tab")
        s_dstf = sem("s_dstf")
        s_iota = sem("s_iota")
        s_ha = sem("s_ha")
        s_hs = sem("s_hs")
        s_hc = sem("s_hc")
        s_hr = sem("s_hr")
        s_hl = sem("s_hl")
        s_hw = sem("s_hw")
        s_dh = sem("s_dh")
        s_q = sem("s_q")
        s_oh = sem("s_oh")
        s_hist = sem("s_hist")
        s_pre = sem("s_pre")
        s_roff = sem("s_roff")
        s_bad = sem("s_bad")
        s_badp = sem("s_badp")
        s_flag = sem("s_flag")
        s_pad = sem("s_pad")
        s_lod = sem("s_lod")

        s_idx = sem("s_idx")
        s_xg = [sem(f"s_xg{i}") for i in range(WINS)]
        s_ht = [sem(f"s_ht{i}") for i in range(2)]
        s_xt = sem("s_xt")
        s_xtc = sem("s_xtc")
        s_coef = sem("s_coef")
        s_prod = sem("s_prod")
        s_mt = sem("s_mt")
        s_mtc = sem("s_mtc")
        s_m = sem("s_m")
        s_mc = sem("s_mc")
        s_ms = [sem(f"s_ms{i}") for i in range(2)]
        s_win = [sem(f"s_win{i}") for i in range(WINS)]
        s_xn = [sem(f"s_xn{i}") for i in range(WINS)]
        s_dl = sem("s_dl")
        s_mask = sem("s_mask")
        s_agg = sem("s_agg")
        s_y = sem("s_y")
        s_yv = sem("s_yv")
        s_st = sem("s_st")
        s_sm = sem("s_sm")
        s_dif = sem("s_dif")
        s_sq = sem("s_sq")
        s_sqp = sem("s_sqp")
        s_tot = sem("s_tot")
        s_std = sem("s_std")
        s_rs = sem("s_rs")
        s_nm = sem("s_nm")
        s_norm = sem("s_norm")
        s_out = [sem(f"s_out{i}") for i in range(WINS)]

        s_cpy = sem("s_cpy")
        s_gtri = sem("s_gtri")
        s_gy = sem("s_gy")
        s_gm = sem("s_gm")
        s_gi = sem("s_gi")
        s_gg = sem("s_gg")
        s_gt = sem("s_gt")
        s_ge = sem("s_ge")
        s_gl = sem("s_gl")
        s_gc = sem("s_gc")
        s_gx = sem("s_gx")
        s_ga = sem("s_ga")
        s_gs = sem("s_gs")
        s_gsc = sem("s_gsc")

        block = ctx.enter_context(nc.Block())

        def prologue_sp(sp):
            sp.wait_ge(s_zero, 1)
            sp.dma_start(dh[:, 0:DC], dst.rearrange("(p c) -> p c", c=DC)).then_inc(s_dh, 16)
            sp.dma_start(dh[0:DP - 1, DC:DC + 1], dst[DC:N_EDGES].rearrange("(p c) -> p c", c=DC)[:, 0:1],
                         allow_slow_non_contiguous=True).then_inc(s_dh, 16)
            sp.dma_start(cst_sb[:, :], cst[:, :]).then_inc(s_cst, 16)
            sp.dma_start(ha[0:90, :], attrT.rearrange("j (r c) -> (j r) c", c=AP_COLS)).then_inc(s_ha, 16)
            sp.dma_start(ha[90:100, :], attrT[6:7, :].rearrange("j (r c) -> (j r) c", c=AP_COLS)).then_inc(s_ha, 16)
            sp.wait_ge(s_zero, 2)
            sp.dma_start(src_tab[:, 0:E_FULL], srcT[:, :]).then_inc(s_tab, 16)
            sp.dma_start(src_tab[0:E_TAIL, E_FULL:E_FULL + 1], src_tail[:, :]).then_inc(s_tab, 16)
            sp.dma_start(dst_tab[:, 0:E_FULL], dstT[:, :]).then_inc(s_tab, 16)
            sp.dma_start(dst_tab[0:E_TAIL, E_FULL:E_FULL + 1], dst_tail[:, :]).then_inc(s_tab, 16)
            sp.dma_start(gsel_f[:, :], gsel[:, :]).then_inc(s_gsel, 16)
            sp.wait_ge(s_wz, 1)
            sp.dma_start(w_raw[0:MUL, 0:MUL], w0[:, 0, :]).then_inc(s_w, 16)
            sp.dma_start(w_raw[0:MUL, MUL:2 * MUL], w1[:, 0, :]).then_inc(s_w, 16)
            for i in range(3):
                sp.dma_start(w_raw[MUL + i:P:3, 0:MUL], w3[:, 0, :]).then_inc(s_w, 16)
                sp.dma_start(w_raw[MUL + i:P:3, MUL:2 * MUL], w4[:, 0, :]).then_inc(s_w, 16)
                sp.dma_start(w_raw[MUL + i:P:3, (2 + i) * MUL:(3 + i) * MUL], w2[:, 0, :]).then_inc(s_w, 16)
            harmonics_sp(sp, 0)

        def harmonics_sp(sp, i):
            for part in range(PARTS):
                if part < 2:
                    sp.wait_ge(s_hc, 2 * i + part + 1)
                else:
                    sp.wait_ge(s_hl, i + 1)
                rows = harm_d[part * COEF:(part + 1) * COEF, :].rearrange("j (r c) -> (j r) c", c=AP_COLS)
                sp.dma_start(rows[:, PIECES[i]], hp[part][:, PIECES[i]]).then_inc(s_hw, 16)
            sp.wait_ge(s_hw, 16 * PARTS * (i + 1))

        def windows_sp(sp):
            sp.wait_ge(s_pad, 1)
            sp.dma_start(msg_d[0:P, :], win[:, 0, 0, :]).then_inc(s_pad, 16)
            sp.wait_ge(s_pad, 17)
            sp.wait_ge(s_flag, 1)
            sp.dma_start(lo_d.rearrange("a (p c) -> (a p) c", c=HB // 2), lo_i[:, :]).then_inc(s_lod, 16)
            sp.wait_ge(s_lod, 16)
            sp.dma_start(lo_row[:, :], lo_d[:, :]).then_inc(s_lod, 16)
            sp.wait_ge(s_lod, 32)

        def prologue_pool(pool):
            g = nc.gpsimd
            g.iota(iota_b[:, :, :], pattern=[[1, HB], [0, HCH]], base=0, channel_multiplier=0,
                   allow_small_or_imprecise_dtypes=True).then_inc(s_iota, 1)
            g.iota(iota_f[:, :], pattern=[[1, P]], base=0, channel_multiplier=0, allow_small_or_imprecise_dtypes=True)
            g.iota(node_base[:, :], pattern=[[P, NO * OT]], base=0, channel_multiplier=0,
                   allow_small_or_imprecise_dtypes=True)
            g.iota(bound[:, :], pattern=[[QE, HB // OT], [0, OT]], base=(STORED + 1) * QE - P,
                   channel_multiplier=QE * HB // OT, allow_small_or_imprecise_dtypes=True)
            g.memset(upper[:, :], 1.0).then_inc(s_iota, 1)
            pool.wait_ge(s_iota, 2)
            g.affine_select(out=upper[:, :], in_=upper[:, :], compare_op=ALU.is_gt, fill=0.0, base=0,
                            pattern=[[1, HB]], channel_multiplier=-1).then_inc(s_iota, 1)
            g.memset(quarter[:, :], float(P // 4)).then_inc(s_iota, 1)

        def prologue_act(act):
            for i, piece in enumerate(PIECES):
                act.wait_ge(s_hs, i + 1)
                nc.scalar.copy(hp[0][:, piece], ha[:, piece]).then_inc(s_hc, 1)
                if i == 0:
                    act_transposed(act, 0, 0)
                act.wait_ge(s_hr, i + 1)
                nc.scalar.copy(hp[1][:, piece], ha[:, piece]).then_inc(s_hc, 1)

        def one_hots(dve, ch):
            v = nc.vector
            need(dve, s_hist, ch - 1)
            for d in range(2):
                last = v.tensor_tensor(
                    oh[:, ch % 2, d, :, :], iota_b[:, :, :],
                    qb[:, d, ch * HCH:(ch + 1) * HCH].unsqueeze(1).to_broadcast([DP, HB, HCH]), ALU.is_equal)
            last.then_inc(s_oh, 1)

        def prologue_dve(dve):
            v = nc.vector
            v.memset(dh[:, :], NO_NODE).then_inc(s_zero, 1)
            v.memset(src_tab[:, :], 0)
            v.memset(dst_tab[:, :], NO_NODE).then_inc(s_zero, 1)
            v.memset(w_raw[:, :], 0.0).then_inc(s_wz, 1)
            v.memset(win[:, 0, 0, :], -1.0).then_inc(s_pad, 1)
            v.memset(eps_sb[:, :], EPS)
            v.memset(ones_sb[:, :], 1.0)
            v.memset(badc[:, :], 0.0).then_inc(s_pre, 1)
            dve.wait_ge(s_dh, 32)
            v.tensor_scalar(qi[:, 0, :], dh[:, 0:DC], 12, None, ALU.logical_shift_right)
            v.tensor_scalar(qi[:, 1, :], dh[:, 0:DC], 7, HB - 1, ALU.logical_shift_right,
                            ALU.bitwise_and).then_inc(s_q, 1)
            dve.wait_ge(s_q, 1)
            v.tensor_copy(qb[:, :, :], qi[:, :, :]).then_inc(s_q, 1)
            dve.wait_ge(s_iota, 1)
            dve.wait_ge(s_q, 2)

            def scale(i):
                v.tensor_scalar(ha[:, PIECES[i]], ha[:, PIECES[i]], a_scale, None, ALU.mult).then_inc(s_hs, 1)

            def rest(i):
                dve.wait_ge(s_hc, 2 * i + 1)
                v.tensor_tensor(ha[:, PIECES[i]], ha[:, PIECES[i]], hp[0][:, PIECES[i]], ALU.subtract).then_inc(s_hr, 1)

            def third(i):
                dve.wait_ge(s_hc, 2 * i + 2)
                v.tensor_tensor(hp[2][:, PIECES[i]], ha[:, PIECES[i]], hp[1][:, PIECES[i]],
                                ALU.subtract).then_inc(s_hl, 1)

            one_hots(dve, 0)
            dve.wait_ge(s_cst, 16)
            dve.wait_ge(s_ha, 32)
            scale(0)
            one_hots(dve, 1)
            rest(0)
            scale(1)
            dve.wait_ge(s_tab, 64)
            v.tensor_copy(dstf_tab[:, :], dst_tab[:, :]).then_inc(s_dstf, 1)
            dve.wait_ge(s_gsel, 16)
            v.tensor_copy(gsel_sb[:, :], gsel_f[:, :])
            dve.wait_ge(s_w, 16 * 11)
            v.tensor_tensor(w_sb[:, :], w_raw[:, :], w_scale, ALU.mult).then_inc(s_wsc, 1)
            third(0)
            rest(1)
            one_hots(dve, 2)
            one_hots(dve, 3)
            third(1)

        def windows_dve(dve):
            v = nc.vector
            dve.wait_ge(s_iota, 4)
            v.tensor_tensor(bad[:, :], dh[:, 0:DC], dh[:, 1:DC + 1], ALU.is_gt).then_inc(s_pre, 1)
            dve.wait_ge(s_pre, 2)
            v.tensor_reduce(badc[0:DP, 0:1], bad[:, :], AXX, ALU.add).then_inc(s_pre, 1)
            dve.wait_ge(s_hist, DC // HCH)
            v.tensor_copy(hist[:, :], pro_ps[0:HB, 0:HB])
            v.tensor_copy(pre[:, 0, :], pro_ps[0:HB, 0:HB])
            v.tensor_reduce(rowsum[:, :], pro_ps[0:HB, 0:HB], AXX, ALU.add).then_inc(s_pre, 1)
            dve.wait_ge(s_pre, 4)
            a, step, n = 0, 1, 4
            while step < HB:
                v.tensor_copy(pre[:, 1 - a, 0:step], pre[:, a, 0:step])
                v.tensor_tensor(pre[:, 1 - a, step:HB], pre[:, a, step:HB], pre[:, a, 0:HB - step],
                                ALU.add).then_inc(s_pre, 1)
                a, step, n = 1 - a, 2 * step, n + 1
                dve.wait_ge(s_pre, n)
            v.tensor_tensor(lo_f[:, :], pre[:, a, :], hist[:, :], ALU.subtract).then_inc(s_pre, 1)
            dve.wait_ge(s_roff, 1)
            v.tensor_copy(roff[:, :], pro_ps[0:HB, 64:65]).then_inc(s_pre, 1)
            dve.wait_ge(s_pre, n + 2)
            v.tensor_scalar(lo_f[:, :], lo_f[:, :], roff[:, 0:1], None, ALU.add).then_inc(s_pre, 1)
            dve.wait_ge(s_pre, n + 3)
            v.tensor_copy(lo_i[:, :], lo_f[:, :].rearrange("p (c two) -> p c two", two=2)[:, :, 1])
            v.tensor_scalar(bad2[:, 0, :], hist[:, :], float(P), None, ALU.is_gt)
            v.tensor_tensor(bad2[:, 1, :], lo_f[:, :], bound[:, :], ALU.is_gt).then_inc(s_pre, 1)
            dve.wait_ge(s_pre, n + 4)
            v.tensor_reduce(badc[0:HB, 1:2], bad2[:, :, :].rearrange("p a b -> p (a b)"), AXX,
                            ALU.add).then_inc(s_bad, 1)
            dve.wait_ge(s_badp, 1)
            v.tensor_scalar(flag[:, :], pro_ps[0:1, 96:97], float(FORCE), None, ALU.add).then_inc(s_flag, 1)

        def histogram_pe(pe, chunks):
            for ch in chunks:
                pe.wait_ge(s_oh, ch + 1)
                for c in range(HCH):
                    last = nc.tensor.matmul(pro_ps[0:HB, 0:HB], oh[:, ch % 2, 0, :, c], oh[:, ch % 2, 1, :, c],
                                            start=(ch == 0 and c == 0), stop=(ch == DC // HCH - 1 and c == HCH - 1))
                last.then_inc(s_hist, 1)

        def windows_pe(pe):
            pe.wait_ge(s_pre, 4)
            nc.tensor.matmul(pro_ps[0:HB, 64:65], upper[:, :], rowsum[:, :], start=True, stop=True).then_inc(s_roff, 1)
            pe.wait_ge(s_bad, 1)
            nc.tensor.matmul(pro_ps[0:1, 96:97], badc[:, 0:1], ones_sb[:, :], start=True, stop=False)
            nc.tensor.matmul(pro_ps[0:1, 96:97], badc[:, 1:2], ones_sb[:, :], start=False,
                             stop=True).then_inc(s_badp, 1)

        def exists(at, off, n):
            return 0 <= at + off < n

        def side(s, off=0):
            return (s + off) % 2

        def pool_gather(pool, q0, s):
            first = fixed(pool, (q0 + s) * QT)
            free, made = count(pool, q0 + s + 1 - WINS), count(pool, q0 + s + 1)
            b = s % WINS
            pool.wait_ge(s_tab, 64)
            need(pool, s_xt, free)
            nc.gpsimd.tensor_copy(idx[:, b, :], src_tab[:, bass.ds(first, QT)]).then_inc(s_idx, 1)
            pool.wait_ge(s_tab, 64)
            pool.wait_ge(s_idx, made)
            for t in range(QT):
                pool.indirect_dma_start(
                    out=xg[:, b, t, :], out_offset=None, in_=x[:, :],
                    in_offset=bass.IndirectOffsetOnAxis(ap=idx[:, b, t:t + 1], axis=0),
                    bounds_check=N_NODES - 1, oob_is_err=False).then_inc(s_xg[b], 16)

        def pool_slot(pool, q0, s, at, nodes):
            o = q0 + s - LAG
            if nodes and exists(at, s - LAG + 1, NO):
                hn, w = side(s, 1 - LAG), (s + 1 - LAG) % WINS
                first, made = fixed(pool, (o + 1) * OT), count(pool, o)
                need(pool, s_mask, made)
                pool.wait_ge(s_win[w], turns(q0, s - LAG + 1, 16 * OT // 2, WINS))
                nc.gpsimd.tensor_tensor(dloc[:, hn, :], win[:, w, :, P], node_base[:, bass.ds(first, OT)],
                                        ALU.subtract).then_inc(s_dl, 1)
            if exists(at, s + 3, NQ):
                pool_gather(pool, q0, s + 3)
            if nodes and exists(at, s - LAG - 1, NO):
                ln_var(pool, side(s, -LAG - 1), q0 + s - LAG - 1)

        def pe_transpose(pe, q0, s):
            b = s % WINS
            pe.wait_ge(s_xg[b], turns(q0, s, 16 * QT, WINS))
            need(pe, s_xtc, q0 + s)
            for t in range(QT):
                last = nc.tensor.transpose(xt_ps[:, t * P:(t + 1) * P], xg[:, b, t, :], ident)
            last.then_inc(s_xt, 1)

        def pe_coef(pe, q0, s, blocks):
            for c in blocks:
                if c == 0:
                    pe.wait_ge(s_ht[s % WINS // 2], turns(q0, s, 16, WINS))
                need(pe, s_prod, 5 * (q0 + s) + (-1, 0, -2, 1, 2)[c])
                nc.tensor.matmul(c_ps[c % 3][:, :], gsel_sb[:, c * P:(c + 1) * P],
                                 ht[:, s % WINS * QE:(s % WINS + 1) * QE], start=True, stop=True).then_inc(s_coef, 1)

        def pe_slot(pe, q0, s, at, nodes):
            q = q0 + s
            o = q - LAG
            h, ho, xo = side(s), side(s, -LAG), (s - LAG) % WINS * OT
            node = nodes and exists(at, s - LAG, NO)
            if at + s == 0:
                pe_coef(pe, 0, 0, range(0, 3))
            if exists(at, s - 2, NQ):
                pe.wait_ge(s_mtc, q - 1)
                need(pe, s_mc, q - 2)
                for t in range(QT):
                    last = nc.tensor.transpose(m_ps[:, t * P:(t + 1) * P], mts[:, t * P:(t + 1) * P], perm)
                last.then_inc(s_m, 1)
            if exists(at, s - 1, NQ):
                pe.wait_ge(s_prod, 5 * q)
                need(pe, s_mtc, q - 1)
                for c in range(4):
                    wc = w_sb[:, 0:MUL] if c == 0 else w_sb[:, MUL:2 * MUL]
                    nc.tensor.matmul(mt_ps[c * MUL:(c + 1) * MUL, :], wc, prod[:, 1 - h, c, :], start=True,
                                     stop=(c == 0), tile_position=(0, c * MUL))
                for c in range(1, 4):
                    last = nc.tensor.matmul(mt_ps[c * MUL:(c + 1) * MUL, :], w_sb[:, (1 + c) * MUL:(2 + c) * MUL],
                                            prod[:, 1 - h, 4, :], start=False, stop=True, tile_position=(0, c * MUL))
                last.then_inc(s_mt, 1)
            if exists(at, s, NQ):
                pe_coef(pe, q0, s, (3, 4))
            if node:
                pe.wait_ge(s_xn[(s - LAG) % WINS],
                           turns(q0, s - LAG, 16, WINS) + (16 if at + s - LAG == NO - 1 else 0))
                for i in range(0, OT, QT):
                    need(pe, s_y, 2 * o - 1 + i // QT)
                    if i:
                        need(pe, s_yv, o)
                    end = min(i + QT, PE_TILES)
                    nc.tensor.matmul(agg_ps[:, i:end, :], ident, xn[:, xo + i:xo + end, :], start=True, stop=False)
            if exists(at, s + 1, NQ):
                pe_transpose(pe, q0, s + 1)
            if node:
                pe.wait_ge(s_mask, o + 1)
            for j in range(OT):
                if j in (2, 4, 6) and exists(at, s + 1, NQ):
                    pe_coef(pe, q0, s + 1, (j // 2 - 1,))
                if node:
                    last = nc.tensor.matmul(agg_ps[:, j, :], mask[:, ho, j, :], win[:, (s - LAG) % WINS, j, 0:P],
                                            start=(j >= PE_TILES), stop=(j in (QT - 1, PE_TILES - 1) or j >= PE_TILES))
                    if j % QT == QT - 1:
                        last.then_inc(s_agg, 1)

        def ln_stats(yt, sl, tiles):
            for j in tiles:
                last = nc.vector.bn_stats(st[:, sl, j, :], yt[:, j, :])
            return last

        def ln_var(pool, sl, n):
            g = nc.gpsimd
            need(pool, s_std, n)
            pool.wait_ge(s_st, n + 1)
            g.tensor_tensor(dif[:, :], st[:, sl, :, 1], st[:, sl, :, 4], ALU.subtract).then_inc(s_dif, 1)
            g.tensor_tensor(m2[:, :], st[:, sl, :, 2], st[:, sl, :, 5], ALU.add)
            g.tensor_tensor(msum[:, sl, :], st[:, sl, :, 1], st[:, sl, :, 4], ALU.add).then_inc(s_sm, 1)
            pool.wait_ge(s_dif, n + 1)
            g.tensor_tensor(sq[:, :], dif[:, :], dif[:, :], ALU.mult).then_inc(s_sq, 1)
            pool.wait_ge(s_sq, n + 1)
            g.tensor_tensor(sqp[:, :], sq[:, :], quarter[:, :], ALU.mult).then_inc(s_sqp, 1)
            pool.wait_ge(s_sm, n + 1)
            pool.wait_ge(s_sqp, n + 1)
            g.tensor_tensor(tot[:, :], m2[:, :], sqp[:, :], ALU.add).then_inc(s_tot, 1)

        def ln_scale(dve, sl, n):
            dve.wait_ge(s_std, n + 1)
            nc.vector.reciprocal(rstd[:, sl, :], std[:, :]).then_inc(s_rs, 1)

        def ln_shift(dve, sl, n):
            dve.wait_ge(s_sm, n + 1)
            dve.wait_ge(s_rs, n + 1)
            nc.vector.scalar_tensor_tensor(nmr[:, sl, :], msum[:, sl, :], -0.5, rstd[:, sl, :],
                                           ALU.mult, ALU.mult).then_inc(s_nm, 1)

        def ln_std(act, n):
            act.wait_ge(s_tot, n + 1)
            nc.scalar.activation(std[:, :], tot[:, :], ACT.Sqrt, bias=eps_sb[:, :], scale=1.0 / P).then_inc(s_std, 1)

        def ln_apply(ot, yt, sl, tiles):
            for j in tiles:
                last = nc.scalar.activation(ot[:, j, :], yt[:, j, :], ACT.Identity, bias=nmr[:, sl, j:j + 1],
                                            scale=rstd[:, sl, j:j + 1])
            return last

        def dve_slot(dve, q0, s, at, nodes):
            q = q0 + s
            o = q - LAG
            v = nc.vector
            h, hn, h1, h2 = side(s), side(s, 1 - LAG), side(s, -LAG - 1), side(s, -LAG - 2)
            y1 = (s - LAG - 1) % WINS
            norm = nodes and exists(at, s - LAG - 2, NO)
            more, stats = nodes and exists(at, s - LAG + 1, NO), nodes and exists(at, s - LAG - 1, NO)
            for c in range(TERMS):
                if stats and c == 2:
                    w1 = y1 * OT + PE_TILES
                    dve.wait_ge(s_agg, 2 * o)
                    dve.wait_ge(s_y, 2 * o)
                    dve.wait_ge(s_xn[y1], turns(q0, s - LAG - 1, 16, WINS) + (16 if at + s - LAG == NO else 0))
                    v.tensor_tensor(y[:, y1, PE_TILES:OT, :], xn[:, w1:w1 + OT - PE_TILES, :],
                                    agg_ps[:, PE_TILES:OT, :], ALU.add).then_inc(s_yv, 1)
                if norm and c == 3:
                    need(dve, s_norm, o - 3)
                    ln_scale(dve, h2, o - 2)
                if norm and c == 4:
                    ln_shift(dve, h2, o - 2)
                if exists(at, s, NQ):
                    if c == 0:
                        dve.wait_ge(s_xtc, q + 1)
                        need(dve, s_mt, q - 1)
                    dve.wait_ge(s_coef, 5 * q + c + 1)
                    v.tensor_tensor(prod[:, h, c, :], xts[:, h, :], c_ps[c % 3][:, :], ALU.mult).then_inc(s_prod, 1)
            if stats:
                dve.wait_ge(s_yv, o)
                ln_stats(y[:, y1, :, :], h1, range(OT)).then_inc(s_st, 1)
            if more:
                need(dve, s_agg, 2 * o)
                dve.wait_ge(s_dl, o + 2)
                v.tensor_tensor(mask[:, hn, :, :], iota_f[:, :].unsqueeze(1).to_broadcast([P, OT, P]),
                                dloc[:, hn, :].unsqueeze(2).to_broadcast([P, OT, P]), ALU.is_equal).then_inc(s_mask, 1)

        def oct_io(eng, first, last, dram, load, buf, done):
            def move(rows, tile):
                eng.dma_start(*((tile, rows) if load else (rows, tile))).then_inc(done, 16)
            if not last:
                move(dram[bass.ds(first, OT * P), :].rearrange("(j p) d -> p j d", p=P), buf)
                return
            first = (NO - 1) * OT * P
            full = (N_NODES - first) // P
            rest = N_NODES - first - full * P
            move(dram[first:first + full * P, :].rearrange("(j p) d -> p j d", p=P), buf[:, 0:full, :])
            move(dram[first + full * P:N_NODES, :], buf[0:rest, full, :])

        def act_transposed(act, q0, s):
            need(act, s_prod, 5 * (q0 + s - 1))
            act.wait_ge(s_xt, q0 + s + 1)
            nc.scalar.copy(xts[:, side(s), :], xt_ps[:, :]).then_inc(s_xtc, 1)

        def act_slot(act, q0, s, at, nodes):
            q = q0 + s
            o = q - LAG
            h, h3 = side(s), side(s, -LAG - 3)
            yo, y3 = (s - LAG) % WINS, (s - LAG - 3) % WINS
            norm = nodes and exists(at, s - LAG - 3, NO)
            if nodes and exists(at, s - LAG - 2, NO):
                ln_std(act, o - 2)
            if exists(at, s - 2, NQ):
                act.wait_ge(s_m, q - 1)
                need(act, s_ms[h], turns(q0, s - 4, 16))
                act.wait_ge(s_dstf, 1)
                nc.scalar.copy(mrow[:, h, :, P], dstf_tab[:, bass.ds((q - 2) * QT, QT)])
                nc.scalar.copy(mrow[:, h, :, 0:P], m_ps[:, :].rearrange("p (t f) -> p t f", f=P)).then_inc(s_mc, 1)
            if norm:
                if exists(at, s - LAG - 7, NO):
                    act.wait_ge(s_out[y3], turns(q0, s - LAG - 7, 16, WINS))
                act.wait_ge(s_nm, o - 2)
                ln_apply(on[:, y3, :, :], y[:, y3, :, :], h3, range(0, OT // 2))
            if exists(at, s - 1, NQ):
                need(act, s_m, q - 1)
                act.wait_ge(s_mt, q)
                nc.scalar.copy(mts[:, :], mt_ps[:, :]).then_inc(s_mtc, 1)
            if norm:
                ln_apply(on[:, y3, :, :], y[:, y3, :, :], h3, range(OT // 2, OT)).then_inc(s_norm, 1)
            if exists(at, s + 1, NQ):
                act_transposed(act, q0, s + 1)
            if exists(at, s - 2, NQ):
                rows = fixed(act, P + (q - 2) * QE)
                act.wait_ge(s_mc, q - 1)
                act.dma_start(msg_d[bass.ds(rows, QE), :].rearrange("(t p) d -> p t d", p=P),
                              mrow[:, h, :, :]).then_inc(s_ms[h], 16)
            if nodes and exists(at, s - LAG, NO):
                need(act, s_norm, o - 3)
                for i in range(0, OT, QT):
                    act.wait_ge(s_agg, 2 * o + 1 + i // QT)
                    end = min(i + QT, PE_TILES)
                    nc.scalar.copy(y[:, yo, i:end, :], agg_ps[:, i:end, :]).then_inc(s_y, 1)

        def sp_slot(sp, q0, s, at, nodes):
            q = q0 + s
            o = q - LAG
            h, w = side(s), (s + 3 - LAG) % WINS
            if nodes and exists(at, s - LAG + 3, NO):
                _, los = nc.values_load_multi_w_load_instructions(
                    lo_row[0:1, bass.ds((o + 3) * (OT // 2), OT // 2)], engines=[mybir.EngineType.SP], min_val=0,
                    max_val=N_EDGES, skip_runtime_bounds_check_because="a sum of a histogram of N_EDGES edges")
                stored = count(sp, turns(q0, s - 3, 16)) if exists(at, s - 3, NQ) else 16 * (NQ // 2)
                stored2 = count(sp, turns(q0, s - 4, 16)) if exists(at, s - 4, NQ) else 16 * (NQ // 2)
                used = count(sp, 2 * o)
                sp.wait_ge(s_ms[1 - h], stored)
                sp.wait_ge(s_ms[h], stored2)
                need(sp, s_agg, used)
                for i in range(OT // 2):
                    sp.dma_start(win[:, w, 2 * i:2 * i + 2, :], msg_d[bass.ds(los[i], 2 * P), :].rearrange(
                        "(t p) d -> p t d", p=P)).then_inc(s_win[w], 16)
            if nodes and exists(at, s - LAG + 2, NO):
                rows, used, added = fixed(sp, (o + 2) * OT * P), count(sp, 2 * o - 2), count(sp, o - 1)
                need(sp, s_agg, used)
                need(sp, s_yv, added)
                xo = (s + 2 - LAG) % WINS
                oct_io(sp, rows, at + s - LAG + 2 == NO - 1, x, True, xn[:, xo * OT:(xo + 1) * OT, :], s_xn[xo])
            if nodes and exists(at, s - LAG - 4, NO):
                rows, y4 = fixed(sp, (o - 4) * OT * P), (s - LAG - 4) % WINS
                sp.wait_ge(s_norm, count(sp, o - 3))
                oct_io(sp, rows, at + s - LAG - 4 == NO - 1, out, False, on[:, y4, :, :], s_out[y4])
            if exists(at, s + 3, NQ) and s % 2:
                cols, first = fixed(sp, (q + 3) * QE), (s + 3) % WINS
                sp.wait_ge(s_coef, 5 * q + 5)
                width = min(2 * QE, N_EDGES - cols) if isinstance(cols, int) else 2 * QE
                sp.dma_start(ht[:, first * QE:first * QE + width],
                             harm_d[:, bass.ds(cols, width)]).then_inc(s_ht[first // 2], 16)

        SHARED = LAG - 3

        def straight(eng, slot, nodes, first, end):
            for q in range(first, end):
                slot(eng, q - q % WINS, q % WINS, q - q % WINS, nodes)

        def run(eng, slot, nodes):
            lead, tail = 4 * WINS, (NQ - 4) // WINS * WINS
            straight(eng, slot, nodes, SHARED, lead)
            with eng.Fori(lead, tail - WINS + 1, WINS) as q0:
                for s in range(WINS):
                    slot(eng, q0, s, lead, nodes)
            straight(eng, slot, nodes, tail, NQ + (LAG + 4 if nodes else 2))

        NT = E_PAD // P
        edge_m = win[:, 0, 0, 0:P]
        edge_d = win[:, 0, 0, P:P + 1]
        d_wide, same, earlier, below = (mask[:, 0, i, :] for i in range(4))
        rows_y = xn[:, 0, :]
        CP = 125

        def general_sp(sp):
            sp.dma_start(out.rearrange("(a b) d -> a (b d)", b=CP),
                         x.rearrange("(a b) d -> a (b d)", b=CP)).then_inc(s_cpy, 16)
            sp.wait_ge(s_ms[0], 16 * (NQ // 2))
            sp.wait_ge(s_ms[1], 16 * (NQ // 2))

            def load(t, last):
                rows = fixed(sp, P + t * P)
                need(sp, s_gsc, last)
                sp.dma_start(win[:, 0, 0, :], msg_d[bass.ds(rows, P), :]).then_inc(s_gm, 16)
            load(0, 0)
            with sp.Fori(1, NT) as t:
                load(t, count(sp, t * 16))

            def normalise(o, is_last):
                rows, stored, n = fixed(sp, o * OT * P), count(sp, o * 16), count(sp, o + 1)
                need(sp, s_out[0], stored)
                oct_io(sp, rows, is_last, out, True, y[:, 0, :, :], s_xn[0])
                sp.wait_ge(s_norm, n)
                oct_io(sp, rows, is_last, out, False, on[:, 0, :, :], s_out[0])
            sp.wait_ge(s_gsc, 16 * NT)
            normalise(0, False)
            with sp.Fori(1, NO - 1) as o:
                normalise(o, False)
            normalise(NO - 1, True)
            sp.wait_ge(s_out[0], 16 * (NO + 1))

        def general_pool(pool):
            nc.gpsimd.memset(below, 1.0).then_inc(s_gtri, 1)
            pool.wait_ge(s_gtri, 1)
            nc.gpsimd.affine_select(out=below, in_=below, compare_op=ALU.is_gt, fill=0.0, base=0,
                                    pattern=[[-1, P]], channel_multiplier=1).then_inc(s_gtri, 1)
            pool.wait_ge(s_cpy, 16)
            with pool.Fori(0, NT) as t:
                n = count(pool, t + 1)
                pool.wait_ge(s_gy, 1)
                pool.wait_ge(s_gi, n)
                pool.indirect_dma_start(out=rows_y, out_offset=None, in_=out[:, :],
                                        in_offset=bass.IndirectOffsetOnAxis(ap=idx[:, 0, 0:1], axis=0),
                                        bounds_check=N_NODES - 1, oob_is_err=False).then_inc(s_gg, 16)
                pool.wait_ge(s_gy, 1)
                pool.wait_ge(s_gx, n)
                pool.wait_ge(s_gs, n)
                pool.indirect_dma_start(out=out[:, :], out_offset=bass.IndirectOffsetOnAxis(ap=idx[:, 1, 0:1], axis=0),
                                        in_=rows_y, in_offset=None,
                                        bounds_check=N_NODES - 1, oob_is_err=False).then_inc(s_gsc, 16)
                pool.wait_ge(s_gsc, t * 16 + 16)
            ln_var(pool, 0, 0)
            with pool.Fori(1, NO) as o:
                ln_var(pool, 0, o)

        def general_pe(pe):
            with pe.Fori(0, NT) as t:
                pe.wait_ge(s_gi, t + 1)
                nc.tensor.transpose(pro_ps[:, :], d_wide, ident).then_inc(s_gt, 1)
                pe.wait_ge(s_ge, t + 1)
                nc.tensor.matmul(agg_ps[:, 0, :], same, edge_m, start=True, stop=True).then_inc(s_ga, 1)

        def general_dve(dve):
            v = nc.vector
            v.memset(rows_y, 0.0).then_inc(s_gy, 1)
            dve.wait_ge(s_gtri, 2)
            with dve.Fori(0, NT) as t:
                dve.wait_ge(s_gm, t * 16 + 16)
                v.tensor_copy(idx[:, 0, 0:1], edge_d)
                v.tensor_copy(d_wide, edge_d.to_broadcast([P, P])).then_inc(s_gi, 1)
                dve.wait_ge(s_gi, t + 1)
                dve.wait_ge(s_gt, t + 1)
                v.tensor_tensor(same, pro_ps[:, :], d_wide, ALU.is_equal).then_inc(s_ge, 1)
                dve.wait_ge(s_ge, t + 1)
                v.tensor_tensor(earlier, same, below, ALU.mult).then_inc(s_gl, 1)
                dve.wait_ge(s_gl, t + 1)
                v.tensor_reduce(dloc[:, 0, 0:1], earlier, AXX, ALU.add).then_inc(s_gc, 1)
                dve.wait_ge(s_gc, t + 1)
                v.scalar_tensor_tensor(idx[:, 1, 0:1], dloc[:, 0, 0:1], float(1 << 17), edge_d, ALU.mult,
                                       ALU.add).then_inc(s_gx, 1)
                dve.wait_ge(s_gg, t * 16 + 16)
                dve.wait_ge(s_ga, t + 1)
                v.tensor_tensor(rows_y, rows_y, agg_ps[:, 0, :], ALU.add).then_inc(s_gs, 1)

            def normalise(o):
                ln_stats(y[:, 0, :, :], 0, range(OT)).then_inc(s_st, 1)
                ln_scale(dve, 0, o)
                ln_shift(dve, 0, o)
            with dve.Fori(0, NO - 1) as o:
                dve.wait_ge(s_xn[0], o * 16 + 16)
                normalise(o)
            dve.wait_ge(s_xn[0], 16 * (NO + 1))
            normalise(NO - 1)

        def general_act(act):
            with act.Fori(0, NO) as o:
                ln_std(act, o)
                act.wait_ge(s_nm, o + 1)
                ln_apply(on[:, 0, :, :], y[:, 0, :, :], 0, range(OT)).then_inc(s_norm, 1)

        def ways(eng, fast, slow):
            eng.wait_ge(s_flag, 1)
            f = eng.value_load(flag[0:1, 0:1], min_val=0, max_val=1 << 20)
            with eng.If(f == 0):
                fast()
            with eng.Else():
                slow()

        @block.sync
        def _(sp):
            prologue_sp(sp)
            for h in range(2):
                sp.dma_start(ht[:, h * 2 * QE:(h + 1) * 2 * QE],
                             harm_d[:, h * 2 * QE:(h + 1) * 2 * QE]).then_inc(s_ht[h], 16)
            harmonics_sp(sp, 1)
            straight(sp, sp_slot, False, 0, SHARED)
            windows_sp(sp)

            def fast():
                run(sp, sp_slot, True)
                for i in range(WINS):
                    sp.wait_ge(s_out[i], 16 * len(range(i, NO, WINS)) + 16 * (i == (NO - 1) % WINS))

            def slow():
                run(sp, sp_slot, False)
                general_sp(sp)
            ways(sp, fast, slow)

        @block.gpsimd
        def _(pool):
            prologue_pool(pool)
            for s in range(3):
                pool_gather(pool, 0, s)
            straight(pool, pool_slot, False, 0, SHARED)

            def slow():
                run(pool, pool_slot, False)
                general_pool(pool)
            ways(pool, lambda: run(pool, pool_slot, True), slow)

        @block.scalar
        def _(act):
            prologue_act(act)
            straight(act, act_slot, False, 0, SHARED)

            def slow():
                run(act, act_slot, False)
                general_act(act)
            ways(act, lambda: run(act, act_slot, True), slow)

        @block.vector
        def _(dve):
            prologue_dve(dve)
            straight(dve, dve_slot, False, 0, 1)
            windows_dve(dve)
            straight(dve, dve_slot, False, 1, SHARED)

            def slow():
                run(dve, dve_slot, False)
                general_dve(dve)
            ways(dve, lambda: run(dve, dve_slot, True), slow)

        @block.tensor
        def _(pe):
            pe.wait_ge(s_cst, 16)
            histogram_pe(pe, range(0, 1))
            pe_transpose(pe, 0, 0)
            histogram_pe(pe, range(1, DC // HCH))
            pe.wait_ge(s_wsc, 1)
            straight(pe, pe_slot, False, 0, 1)
            windows_pe(pe)
            straight(pe, pe_slot, False, 1, SHARED)

            def slow():
                run(pe, pe_slot, False)
                general_pe(pe)
            ways(pe, lambda: run(pe, pe_slot, True), slow)


def wigner_3j(l1, l2, l3):
    import numpy as np
    from math import factorial

    def coeff(j1, m1, j2, m2, j3, m3):
        if m3 != m1 + m2:
            return 0.0
        vmin = int(max(-j1 + j2 + m3, -j1 + m1, 0))
        vmax = int(min(j2 + j3 + m1, j3 - j1 + j2, j3 + m3))
        f = factorial
        c = ((2.0 * j3 + 1.0) * (f(j3 + j1 - j2) * f(j3 - j1 + j2) * f(j1 + j2 - j3) * f(j3 + m3) * f(j3 - m3))
             / (f(j1 + j2 + j3 + 1) * f(j1 - m1) * f(j1 + m1) * f(j2 - m2) * f(j2 + m2))) ** 0.5
        s = 0
        for v in range(vmin, vmax + 1):
            s += ((-1) ** (v + j2 + m2) * (f(j2 + j3 + m1 - v) * f(j1 - m1 + v))
                  / (f(v) * f(j3 - j1 + j2 - v) * f(j3 + m3 - v) * f(v + j1 - j2 - m3)))
        return float(c * s)

    def basis(l):
        q = np.zeros((2 * l + 1, 2 * l + 1), dtype=np.complex128)
        for m in range(-l, 0):
            q[l + m, l + abs(m)] = 1 / np.sqrt(2)
            q[l + m, l - abs(m)] = -1j / np.sqrt(2)
        q[l, l] = 1
        for m in range(1, l + 1):
            q[l + m, l + abs(m)] = (-1) ** m / np.sqrt(2)
            q[l + m, l - abs(m)] = 1j * (-1) ** m / np.sqrt(2)
        return (-1j) ** l * q

    c = np.zeros((2 * l1 + 1, 2 * l2 + 1, 2 * l3 + 1))
    for m1 in range(-l1, l1 + 1):
        for m2 in range(-l2, l2 + 1):
            if abs(m1 + m2) <= l3:
                c[l1 + m1, l2 + m2, l3 + m1 + m2] = coeff(l1, m1, l2, m2, l3, m1 + m2)
    cc = np.einsum("ij,kl,mn,ikn->jlm", basis(l1), basis(l2), np.conj(basis(l3).T), c.astype(np.complex128))
    cr = np.real(cc)
    return cr / np.linalg.norm(cr)


def constants():
    import numpy as np
    neighbors = 10.0
    norm = {0: np.sqrt(1 / (2 * MUL)) / np.sqrt(neighbors), 1: np.sqrt(3 / (3 * MUL)) / np.sqrt(neighbors)}
    w000, w011, w101, w110, w121 = (wigner_3j(*l) for l in ((0, 0, 0), (0, 1, 1), (1, 0, 1), (1, 1, 0), (1, 2, 1)))
    t = np.abs(w121[0, 0, :]).max() or np.abs(w121[0, 1, :]).max()
    w_scale = np.zeros((P, 5 * MUL))
    g = np.zeros((COEF, TERMS, P))
    V = [slice(MUL + i, P, 3) for i in range(3)]
    w_scale[:MUL, :MUL] = norm[0] * w000[0, 0, 0]
    g[0, 0, :MUL] = 1
    w_scale[MUL:, :MUL] = norm[0] * w110[0, 0, 0]
    w_scale[:MUL, MUL:2 * MUL] = norm[1] * w011[0, 0, 0]
    w_scale[MUL:, MUL:2 * MUL] = norm[1] * t
    w_scale[MUL:, 2 * MUL:] = norm[1] * w101[0, 0, 0]
    g[0, 4, MUL:] = 1
    for i in range(3):
        for j in range(3):
            g[1 + j, 0, V[i]] = w110[i, j, 0] / w110[0, 0, 0]
        for k in range(3):
            g[1 + i, 1 + k, :MUL] = w011[0, i, k] / w011[0, 0, 0]
            for j in range(5):
                row, by = (9, np.sqrt(3)) if j == 2 else (4 + j, 1)
                g[row, 1 + k, V[i]] = w121[i, j, k] / t * by
    whole = np.rint(g)
    assert np.abs(g - whole).max() < 1e-9 and np.abs(whole).max() <= 2
    gsel = np.tile(whole.reshape(COEF, TERMS * P), (PARTS, 1)).astype(np.float32)
    ident = np.eye(P)
    perm = np.zeros((P, P))
    perm[np.arange(MUL), np.arange(MUL)] = 1
    for k in range(3):
        for w in range(MUL):
            perm[MUL + k * MUL + w, MUL + 3 * w + k] = 1
    a_scale = np.ones((P, 1))
    a_scale[90:AP_ROWS] = 1 / np.sqrt(3)
    cst = np.concatenate([ident, perm, w_scale, a_scale], axis=1).astype(np.float32)
    return cst, gsel


def host_layout(inputs):
    import numpy as np
    x, src, dst, attr = (np.asarray(inputs[n]) for n in ("x", "src", "dst", "edge_attr_9"))
    full = E_FULL * P
    cst, gsel = constants()
    arrays = {
        "x": x,
        "srcT": src[:full].reshape(E_FULL, P).T, "src_tail": src[full:].reshape(E_TAIL, 1),
        "dst": dst,
        "dstT": dst[:full].reshape(E_FULL, P).T, "dst_tail": dst[full:].reshape(E_TAIL, 1),
        "attrT": attr.T,
        **{f"w{i}": np.asarray(inputs[f"L0_gnn_w{i}"]) for i in range(5)},
        "cst": cst, "gsel": gsel,
    }
    return {n: np.ascontiguousarray(a) for n, a in arrays.items()}


def kernel(**inputs):
    import numpy as _np
    import concourse.bacc as _bacc
    from concourse import mybir as _mybir
    from concourse.bass_utils import run_bass_kernel_spmd as _run

    nc = _bacc.Bacc("TRN2", target_bir_lowering=False, num_devices=1)
    arrays = host_layout(inputs)
    args = [nc.dram_tensor(n, a.shape, _mybir.dt.from_np(a.dtype), kind="ExternalInput").ap()
            for n, a in arrays.items()]
    args.append(nc.dram_tensor("out", (N_NODES, P), _mybir.dt.float32, kind="ExternalOutput").ap())
    build(nc, *args)
    r = _run(nc, [arrays], core_ids=[0])
    return r.results[0]["out"]
```
